# Optimizing a Trainium2 kernel written in Bass

```python
import numpy as np
import jax
import jax.numpy as jnp

def _softmax(x, axis=-1):
    return jax.nn.softmax(x, axis=axis)

def _gelu(x):
    return jax.nn.gelu(x, approximate=True)

def _silu(x):
    return jax.nn.silu(x)

def _sigmoid(x):
    return jax.nn.sigmoid(x)

def _layernorm(x, axis=-1, eps=1e-05):
    m = jnp.mean(x, axis=axis, keepdims=True)
    v = jnp.var(x, axis=axis, keepdims=True)
    return (x - m) / jnp.sqrt(v + eps)

def _scatter_add(tgt, idx, src, axis=0):
    return tgt.at[idx].add(src)

def _segment_sum(src, seg, n):
    return jax.ops.segment_sum(src, seg, n)
kernel_name = 'mk_adj_resnorm_d4_adj_r2_a24ce0'

def setup_inputs(seed: int=0):
    np.random.seed(seed)
    _w = jnp.asarray

    def _rec_inputs():
        import jax
        import jax.numpy as jnp
        _gk = jax.random.key(seed)
        x = -0.0005207 + 1.001 * jax.random.normal(jax.random.fold_in(_gk, 1), (2048, 128), jnp.float32)
        _w = (1.0 + jnp.arange(2048, dtype=jnp.float32)) ** (-0.5)
        _w = _w / _w.mean()
        _pij = jnp.clip(0.0078125 * _w[:, None] * _w[None, :], 0.0, 1.0)
        _a = jax.random.uniform(jax.random.fold_in(_gk, 2), (2048, 2048)) < _pij
        _a = jnp.logical_or(_a, jnp.eye(2048, dtype=bool))
        _af = _a.astype(jnp.float32)
        _af = _af * jax.random.uniform(jax.random.fold_in(_gk, 3), (2048, 2048), jnp.float32, 0.05, 1)
        adj = _af
        return (x, adj)
    x, adj = _rec_inputs()

    def _L0_gnn_setup():
        import jax, jax.numpy as jnp
        import numpy as np
        N = 8192
        F_IN = 128
        F_OUT = 128
        key = jax.random.key(seed)
        k1, k2, k3, k4 = jax.random.split(key, 4)
        features = jax.random.normal(k1, (N, F_IN), dtype=jnp.float32)
        adj = jax.random.uniform(k2, (N, N), dtype=jnp.float32)
        kernel = jax.random.normal(k3, (F_IN, F_OUT), dtype=jnp.float32) * 0.02
        bias = jax.random.normal(k4, (F_OUT,), dtype=jnp.float32) * 0.02
        return {'features': features, 'adj': adj, 'kernel': kernel, 'bias': bias}
    _L0_gnn_all = _L0_gnn_setup()
    _L0_gnn_in = {k: v for k, v in _L0_gnn_all.items() if k in ('kernel', 'bias')}
    del _L0_gnn_all

    def _L1_gnn_setup():
        import jax, jax.numpy as jnp
        import numpy as np
        EPS = 1e-06
        key = jax.random.key(seed)
        k1, k2, k3 = jax.random.split(key, 3)
        N, F_IN, F_OUT = (4096, 128, 128)
        x = jax.random.normal(k1, (N, F_IN), dtype=jnp.float32)
        adj = jax.random.uniform(k2, (N, N), dtype=jnp.float32)
        stdv = 1.0 / np.sqrt(F_OUT)
        weight = jax.random.uniform(k3, (F_IN, F_OUT), dtype=jnp.float32, minval=-stdv, maxval=stdv)
        return {'x': x, 'adj': adj, 'weight': weight}
    _L1_gnn_all = _L1_gnn_setup()
    _L1_gnn_in = {k: v for k, v in _L1_gnn_all.items() if k in ('weight',)}
    del _L1_gnn_all

    def _L2_gnn_setup():
        import jax, jax.numpy as jnp
        import numpy as np
        key = jax.random.key(seed)
        k1, k2, k3, k4 = jax.random.split(key, 4)
        n, in_dim, out_dim = (8192, 128, 128)
        h = jax.random.normal(k1, (n, in_dim), dtype=jnp.float32)
        adj = jax.random.uniform(k2, (n, n), dtype=jnp.float32)
        W_self = jax.random.normal(k3, (in_dim, out_dim), dtype=jnp.float32) * (1.0 / np.sqrt(in_dim))
        W_neigh = jax.random.normal(k4, (in_dim, out_dim), dtype=jnp.float32) * (1.0 / np.sqrt(in_dim))
        return {'h': h, 'adj': adj, 'W_self': W_self, 'W_neigh': W_neigh}
    _L2_gnn_all = _L2_gnn_setup()
    _L2_gnn_in = {k: v for k, v in _L2_gnn_all.items() if k in ('W_self', 'W_neigh')}
    del _L2_gnn_all

    def _L3_gnn_setup():
        import jax, jax.numpy as jnp
        import numpy as np
        LN_EPS = 1e-05
        key = jax.random.key(seed)
        ks = jax.random.split(key, 6)
        N, D = (512, 128)
        return {'node_feats': jax.random.normal(ks[0], (N, D), dtype=jnp.float32), 'adj': jax.random.uniform(ks[1], (N, N), dtype=jnp.float32), 'msg_w': jax.random.normal(ks[2], (D, 2 * D), dtype=jnp.float32) * 0.05, 'msg_b': jax.random.normal(ks[3], (D,), dtype=jnp.float32) * 0.05, 'upd_w': jax.random.normal(ks[4], (D, 2 * D), dtype=jnp.float32) * 0.05, 'upd_b': jax.random.normal(ks[5], (D,), dtype=jnp.float32) * 0.05, 'ln_w': jnp.ones((D,), dtype=jnp.float32), 'ln_b': jnp.zeros((D,), dtype=jnp.float32)}
    _L3_gnn_all = _L3_gnn_setup()
    _L3_gnn_in = {k: v for k, v in _L3_gnn_all.items() if k in ('msg_w', 'msg_b', 'upd_w', 'upd_b', 'ln_w', 'ln_b')}
    del _L3_gnn_all
    return {'x': x, 'adj': adj, 'L0_gnn_kernel': _L0_gnn_in['kernel'], 'L0_gnn_bias': _L0_gnn_in['bias'], 'L1_gnn_weight': _L1_gnn_in['weight'], 'L2_gnn_W_self': _L2_gnn_in['W_self'], 'L2_gnn_W_neigh': _L2_gnn_in['W_neigh'], 'L3_gnn_msg_w': _L3_gnn_in['msg_w'], 'L3_gnn_msg_b': _L3_gnn_in['msg_b'], 'L3_gnn_upd_w': _L3_gnn_in['upd_w'], 'L3_gnn_upd_b': _L3_gnn_in['upd_b'], 'L3_gnn_ln_w': _L3_gnn_in['ln_w'], 'L3_gnn_ln_b': _L3_gnn_in['ln_b']}

def reference(x, adj, L0_gnn_kernel, L0_gnn_bias, L1_gnn_weight, L2_gnn_W_self, L2_gnn_W_neigh, L3_gnn_msg_w, L3_gnn_msg_b, L3_gnn_upd_w, L3_gnn_upd_b, L3_gnn_ln_w, L3_gnn_ln_b):
    import jax
    import jax.numpy as jnp

    def _L0_gnn_ref(features, adj, kernel, bias):
        import jax, jax.numpy as jnp
        import numpy as np
        N = 8192
        F_IN = 128
        F_OUT = 128
        xw = features @ kernel
        out = adj @ xw
        return jax.nn.relu(out + bias)

    def _L1_gnn_ref(x, adj, weight):
        import jax, jax.numpy as jnp
        import numpy as np
        EPS = 1e-06
        N = adj.shape[0]
        a_tilde = adj + jnp.eye(N, dtype=adj.dtype)
        d_inv_sqrt = jax.lax.rsqrt(jnp.sum(adj, axis=1) + EPS)
        adj_norm = d_inv_sqrt[:, None] * a_tilde * d_inv_sqrt[None, :]
        support = x @ weight
        return adj_norm @ support

    def _L2_gnn_ref(h, adj, W_self, W_neigh):
        import jax, jax.numpy as jnp
        import numpy as np
        deg = jnp.clip(jnp.sum(adj, axis=1, keepdims=True), 1.0)
        h_neigh = adj @ h / deg
        return h @ W_self + h_neigh @ W_neigh

    def _L3_gnn_ref(node_feats, adj, msg_w, msg_b, upd_w, upd_b, ln_w, ln_b):
        import jax, jax.numpy as jnp
        import numpy as np
        LN_EPS = 1e-05
        D = node_feats.shape[-1]
        s = node_feats @ msg_w[:, :D].T
        d = node_feats @ msg_w[:, D:].T
        messages = jax.nn.gelu(s[:, None, :] + d[None, :, :] + msg_b, approximate=False)
        aggregated = jnp.einsum('ijd,ij->id', messages, adj)
        combined = jnp.concatenate([node_feats, aggregated], axis=-1)
        new_feats = combined @ upd_w.T + upd_b
        h = jax.nn.gelu(new_feats, approximate=False) + node_feats
        mu = jnp.mean(h, axis=-1, keepdims=True)
        var = jnp.var(h, axis=-1, keepdims=True)
        return (h - mu) / jnp.sqrt(var + LN_EPS) * ln_w + ln_b
    x = _layernorm(x + _L0_gnn_ref(x, adj, L0_gnn_kernel, L0_gnn_bias), axis=-1)
    x = _layernorm(x + _L1_gnn_ref(x, adj, L1_gnn_weight), axis=-1)
    x = _layernorm(x + _L2_gnn_ref(x, adj, L2_gnn_W_self, L2_gnn_W_neigh), axis=-1)
    x = _layernorm(x + _L3_gnn_ref(x, adj, L3_gnn_msg_w, L3_gnn_msg_b, L3_gnn_upd_w, L3_gnn_upd_b, L3_gnn_ln_w, L3_gnn_ln_b), axis=-1)
    return x

_drawn_inputs = setup_inputs


def setup_inputs(seed=0):
    import zlib

    import numpy as np

    out = dict(_drawn_inputs(seed))
    spreads = {'L3_gnn_ln_w': (1.0, 0.2), 'L3_gnn_ln_b': (0.0, 0.1)}
    factors = {'L0_gnn_bias': 3.033, 'L3_gnn_upd_b': 3.86}
    for name, (base, spread) in spreads.items():
        noise = np.random.default_rng([zlib.crc32(name.encode()), seed]).standard_normal(out[name].shape)
        drawn = base * np.exp(spread * noise) if base else spread * noise
        out[name] = jnp.asarray(drawn.astype(out[name].dtype))
    for name, factor in factors.items():
        out[name] = (out[name] * factor).astype(out[name].dtype)
    return out
```

```python
from contextlib import ExitStack

import concourse.bass as bass
from concourse import mybir

ALU = mybir.AluOpType
ACT = mybir.ActivationFunctionType
F32 = mybir.dt.float32
BF16 = mybir.dt.bfloat16
I32 = mybir.dt.int32
AX_X = mybir.AxisListType.X

P = 128
N = 2048
D = 128
T = N // P
NC = 4
CW = N // NC
TC = CW // P
H = 2
HW = N // H
G = 32
NG = N // G
LN_EPS = 1e-5
DEG_EPS = 1e-6
STAGE = 2


def build(nc, x, xT_unused, adj, adjT, w0, b0, w1, w_self, w_neigh, msg_src, msg_dst, msg_b,
          upd_x, upd_agg, upd_b, ln_w, ln_b, out):
    ctx = ExitStack()
    with ctx:
        def sb(name, shape, dt=F32):
            return ctx.enter_context(nc.sbuf_tensor(name, shape, dt))

        def sem(name):
            return ctx.enter_context(nc.semaphore(name))

        adjT_sb = sb("adjT_sb", [P, T, N])
        adj_rows = sb("adj_rows", [P, STAGE, N])
        X = sb("X", [P, T, D])
        U = sb("U", [P, T, D])
        hid = sb("hid", [P, 2, TC, D])
        YT = sb("YT", [P, 2, CW])
        wts = sb("wts", [P, 8, D])
        W0, W1, WSELF, WNEIGH, MSRC, MDST, UPDX, UPDA = range(8)
        rows = sb("rows", [1, 5, D])
        B0, MSGB, UPDB, LNW, LNB = range(5)
        msgb_col = sb("msgb_col", [P, 1])
        ones_row = sb("ones_row", [1, P])
        ident = sb("ident", [P, P])
        sel_bf = sb("sel_bf", [3 * G, G], BF16)
        sel_f = sb("sel_f", [3 * G, G])
        eps_ln = sb("eps_ln", [P, 1])
        eps_deg = sb("eps_deg", [P, 1])
        row_sum = sb("row_sum", [P, T])
        dis = sb("dis", [P, T])
        dis_root = sb("dis_root", [P, T])
        deg = sb("deg", [P, T])
        rdeg = sb("rdeg", [P, T])
        bn6 = sb("bn6", [P, 2, TC, 6])
        mv = sb("mv", [P, 2, TC, 2])
        root = sb("root", [P, 2, TC])
        rstd = sb("rstd", [P, 2, TC])
        lnw_bc = sb("lnw_bc", [P, D])
        lnb_bc = sb("lnb_bc", [P, D])
        pool = adjT_sb[:, :, :].rearrange("p t n -> p (t n)")
        XT = pool[:, 0:N]
        dT = pool[:, N:2 * N]
        sT = pool[:, 2 * N:3 * N]
        accT = pool[:, 3 * N:4 * N]
        gel = pool[:, 4 * N:5 * N].rearrange("p (h n) -> p h n", h=H)
        junk = pool[:, 5 * N:6 * N].rearrange("p (h n) -> p h n", h=H)
        upd = pool[:, 7 * N:8 * N].rearrange("p (t n) -> p t n", t=T)
        fin = pool[:, 6 * N:7 * N].rearrange("p (t n) -> p t n", t=T)
        acc2 = sb("acc2", [P, G, H])
        xs = sb("xs", [3 * G, N])
        parts = sb("parts", [3 * G, 2, N], BF16)
        ps = [ctx.enter_context(nc.psum_tensor(f"ps{i}", [P, CW], F32)) for i in range(4)]
        psB = [ctx.enter_context(nc.psum_tensor(f"psB{i}", [P, HW], F32)) for i in range(H)]
        psZ = [psB[0][:, 0:CW], psB[0][:, CW:HW]]
        psS = [psB[1][:, 0:CW], psB[1][:, CW:HW]]

        XT2 = sb("XT2", [P, N])
        hid2 = sb("hid2", [P, 2, TC, D])

        s_bcln = sem("ln_vectors_broadcast")
        s_w = sem("weights_landed")
        s_x = sem("x_landed")
        s_adjT = [sem(f"adjT_landed{J}") for J in range(T)]
        s_rows = [sem(f"adj_rows_landed{k}") for k in range(STAGE)]
        s_rowsum = sem("row_sum_done")
        s_turn = sem("turn_taken")
        s_const = sem("constants_ready")
        s_dis = sem("dis_ready")
        s_dchain = sem("dve_step")
        s_achain = sem("act_step")
        s_pchain = sem("pool_step")
        s_Y = sem("Y_chunk_ready")
        s_YT = sem("YT_copied")
        s_Z = sem("Z_ready")
        s_hid = sem("hid_ready")
        s_var = sem("variance_ready")
        s_root = sem("root_ready")
        s_X = sem("X_chunk_ready")
        s_XTp = sem("XT_in_psum")
        s_XT = sem("XT_copied")
        s_T3 = sem("dT_sT_in_psum")
        s_T3c = sem("dT_sT_copied")
        s_xs = sem("xs_landed")
        s_split = sem("parts_ready")
        s_rowsdone = sem("parts_used")
        s_bc = [sem(f"adj_row_broadcast{h}") for h in range(H)]
        s_gelu = [sem(f"gelu_ready{h}") for h in range(H)]
        s_used = [sem(f"row_half_summed{h}") for h in range(H)]
        s_acc = sem("accT_ready")
        s_F = sem("final_in_psum")
        s_Fg = sem("final_gelu")
        s_out = sem("out_stored")

        block = ctx.enter_context(nc.Block())

        wlist = [w0, w1, w_self, w_neigh, msg_src, msg_dst, upd_x, upd_agg]
        rlist = [b0, msg_b, upd_b, ln_w, ln_b]
        N_W = 16 * (len(wlist) + len(rlist) + 1)

        @block.sync
        def _(sp):
            sp.dma_start(X[:, :, :], x.rearrange("(t p) d -> p t d", p=P)).then_inc(s_x, 16)
            for J in range(T):
                sp.dma_start(adjT_sb[:, J, :], adjT[J * P:(J + 1) * P, :]).then_inc(s_adjT[J], 16)
                if J >= STAGE:
                    sp.wait_ge(s_rowsum, J - STAGE + 1)
                sp.dma_start(adj_rows[:, J % STAGE, :], adj[J * P:(J + 1) * P, :]).then_inc(s_rows[J % STAGE], 16)
            for part in range(3):
                sp.dma_start(xs[part * G:(part + 1) * G, :], adj[0:G, :]).then_inc(s_xs, 16)
            with sp.Fori(1, NG) as n:
                sp.wait_ge(s_split, n)
                for part in range(3):
                    sp.dma_start(xs[part * G:(part + 1) * G, :], adj[bass.ds(n * G, G), :]).then_inc(s_xs, 16)
            for c in range(NC):
                sp.wait_ge(s_X, 3 * NC + c + 1)
                sp.dma_start(out.rearrange("(t p) d -> p t d", p=P)[:, c * TC:(c + 1) * TC, :],
                             fin[:, c * TC:(c + 1) * TC, :]).then_inc(s_out, 16)
            sp.wait_ge(s_out, 16 * NC)

        @block.gpsimd
        def _(pool_e):
            pool_e.memset(ident[:, :], 0.0).then_inc(s_pchain, 1)
            pool_e.memset(sel_f[:, :], 0.0).then_inc(s_pchain, 1)
            pool_e.memset(ones_row[:, :], 1.0).then_inc(s_const, 1)
            pool_e.memset(eps_ln[:, :], LN_EPS).then_inc(s_const, 1)
            pool_e.memset(eps_deg[:, :], DEG_EPS).then_inc(s_const, 1)
            pool_e.wait_ge(s_pchain, 1)
            pool_e.affine_select(out=ident[:, :], in_=ident[:, :], compare_op=ALU.not_equal, fill=1.0,
                                 base=0, pattern=[[-1, P]], channel_multiplier=1).then_inc(s_const, 1)
            for part in range(3):
                pool_e.wait_ge(s_pchain, 2 + part)
                pool_e.affine_select(out=sel_f[:, :], in_=sel_f[:, :], compare_op=ALU.not_equal, fill=1.0,
                                     base=-part * G, pattern=[[-1, G]], channel_multiplier=1).then_inc(s_pchain, 1)
            pool_e.wait_ge(s_pchain, 5)
            pool_e.tensor_copy(sel_bf[:, :], sel_f[:, :]).then_inc(s_const, 1)

            def split(b, n, first):
                pool_e.wait_ge(s_xs, (n + 1) * 48)
                if not first:
                    pool_e.wait_ge(s_rowsdone, n - 1)
                pool_e.sem_inc(s_turn, 1)
                steps = 5
                c0 = n * 5 + 5

                def link(k, ins):
                    ins.then_inc(s_pchain, 1)
                    pool_e.wait_ge(s_pchain, c0 + k)
                link(1, pool_e.tensor_copy(parts[:, b, :], xs[:, :]))
                link(2, pool_e.tensor_tensor(xs[G:3 * G, :], xs[G:3 * G, :], parts[G:3 * G, b, :], ALU.subtract)) if False else None
                for q in (1, 2):
                    r = slice(q * G, (q + 1) * G)
                    ins = pool_e.tensor_tensor(xs[r, :], xs[r, :], parts[r, b, :], ALU.subtract)
                ins.then_inc(s_pchain, 1)
                pool_e.wait_ge(s_pchain, c0 + 2)
                pool_e.sem_inc(s_turn, 1)
                for q in (1, 2):
                    r = slice(q * G, (q + 1) * G)
                    ins = pool_e.tensor_copy(parts[r, b, :], xs[r, :])
                ins.then_inc(s_pchain, 1)
                pool_e.wait_ge(s_pchain, c0 + 3)
                r = slice(2 * G, 3 * G)
                link(4, pool_e.tensor_tensor(xs[r, :], xs[r, :], parts[r, b, :], ALU.subtract))
                pool_e.sem_inc(s_turn, 1)
                ins = pool_e.tensor_copy(parts[r, b, :], xs[r, :])
                ins.then_inc(s_pchain, 1)
                pool_e.wait_ge(s_pchain, c0 + 5)
                pool_e.sem_inc(s_split, 1)

            split(0, 0, True)
            split(1, 1, True)
            with pool_e.Fori(1, NG // 2) as m:
                split(0, m * 2, False)
                split(1, m * 2 + 1, False)

        @block.scalar
        def _(act):
            for k, w in enumerate(wlist):
                act.dma_start(wts[:, k, :], w).then_inc(s_w, 16)
            for k, r in enumerate(rlist):
                act.dma_start(rows[:, k, :], r).then_inc(s_w, 16)
            act.dma_start(msgb_col[:, :], msg_b.rearrange("a d -> d a")).then_inc(s_w, 16)
            for t in range(T):
                act.wait_ge(s_rows[t % STAGE], 16 * (t // STAGE + 1))
                act.activation(adj_rows[:, t % STAGE, :], adj_rows[:, t % STAGE, :], ACT.Copy,
                               accum_out=row_sum[:, t:t + 1]).then_inc(s_rowsum, 1)
            act.wait_ge(s_const, 5)
            act.wait_ge(s_rowsum, T)
            act.activation(dis_root[:, :], row_sum[:, :], ACT.Sqrt, bias=eps_deg[:, :]).then_inc(s_dis, 1)

            def copy_Y(l, c):
                k = NC * l + c
                act.wait_ge(s_Y, k + 1)
                if k >= 2:
                    act.wait_ge(s_Z, k - 1)
                act.activation(YT[:, k % 2, :], ps[c][:, :], ACT.Copy).then_inc(s_YT, 1)

            def roots(k):
                act.wait_ge(s_var, k + 1)
                act.activation(root[:, k % 2, :], mv[:, k % 2, :, 1], ACT.Sqrt, bias=eps_ln[:, :]).then_inc(s_root, 1)

            def copy_XT(l, c):
                k = NC * l + c
                act.wait_ge(s_XTp, k + 1)
                act.activation(XT2[:, c * CW:(c + 1) * CW] if l == 0 else XT[:, c * CW:(c + 1) * CW],
                               psS[k % 2] if l == 0 else ps[c][:, :], ACT.Copy).then_inc(s_XT, 1)

            for l in range(3):
                if l == 2:
                    for c in range(NC):
                        copy_XT(0, c)
                for c in range(NC):
                    copy_Y(l, c)
                for c in range(NC):
                    roots(NC * l + c)
            for c in range(NC):
                copy_XT(1, c)
            for c in range(NC):
                act.wait_ge(s_T3, 2 * c + 1)
                act.activation(dT[:, c * CW:(c + 1) * CW], psZ[0], ACT.Copy).then_inc(s_T3c, 1)
                act.wait_ge(s_T3, 2 * c + 2)
                act.activation(sT[:, c * CW:(c + 1) * CW], psZ[1], ACT.Identity, bias=msgb_col[:, :]).then_inc(s_T3c, 1)
            act.wait_ge(s_T3c, 2 * NC)
            with act.Fori(0, N) as r:
                for h in range(H):
                    act.wait_ge(s_used[h], r + 1)
                    act.sem_inc(s_turn, 1)
                    act.activation(gel[:, h, :], dT[:, h * HW:(h + 1) * HW], ACT.Gelu,
                                   bias=sT[:, bass.ds(r, 1)]).then_inc(s_gelu[h], 1)
            for c in range(NC):
                act.wait_ge(s_F, c + 1)
                act.activation(upd[:, c * TC:(c + 1) * TC, :].rearrange("p t d -> p (t d)"), ps[c][:, :], ACT.Gelu).then_inc(s_Fg, 1)
            for k in range(3 * NC, 5 * NC):
                roots(k)

        def layer_norm2(dve, link, k, src, dst):
            b = k % 2
            for i in range(TC):
                ins = nc.vector.bn_stats(out=bn6[:, b, i, :], in_=src[:, i, :])
            link(ins)
            for i in range(TC):
                ins = nc.vector.bn_aggr(out=mv[:, b, i, :], in_=bn6[:, b, i, :])
            ins.then_inc(s_var, 1)
            dve.wait_ge(s_root, k + 1)
            link(nc.vector.reciprocal(rstd[:, b, :], root[:, b, :]))
            for i in range(TC):
                ins = nc.vector.tensor_scalar(dst[:, i, :], src[:, i, :], mv[:, b, i, 0:1], rstd[:, b, i:i + 1],
                                              ALU.subtract, ALU.mult)
            return ins

        @block.vector
        def _(dve):
            chain = [0]

            def link(ins):
                chain[0] += 1
                ins.then_inc(s_dchain, 1)
                dve.wait_ge(s_dchain, chain[0])

            dve.wait_ge(s_x, 16)

            def layer_norm(k, dst, scaled=None):
                b = k % 2
                for i in range(TC):
                    ins = nc.vector.bn_stats(out=bn6[:, b, i, :], in_=hid[:, b, i, :])
                link(ins)
                for i in range(TC):
                    ins = nc.vector.bn_aggr(out=mv[:, b, i, :], in_=bn6[:, b, i, :])
                ins.then_inc(s_var, 1)
                dve.wait_ge(s_root, k + 1)
                link(nc.vector.reciprocal(rstd[:, b, :], root[:, b, :]))
                for i in range(TC):
                    ins = nc.vector.tensor_scalar(dst[:, i, :], hid[:, b, i, :], mv[:, b, i, 0:1], rstd[:, b, i:i + 1],
                                                  ALU.subtract, ALU.mult)
                return ins

            for c in range(NC):
                dve.wait_ge(s_Z, c + 1)
                xc = X[:, c * TC:(c + 1) * TC, :]
                link(nc.vector.scalar_tensor_tensor(out=hid[:, c % 2, :, :].rearrange("p t d -> p (t d)"),
                                                    in0=psZ[c % 2], scalar=0.0,
                                                    in1=xc.rearrange("p t d -> p (t d)"), op0=ALU.max, op1=ALU.add))
                if c == 0:
                    dve.wait_ge(s_dis, 1)
                    link(nc.vector.reciprocal(dis[:, :], dis_root[:, :]))
                    link(nc.vector.tensor_scalar(deg[:, :], row_sum[:, :], 1.0, None, ALU.max))
                    link(nc.vector.reciprocal(rdeg[:, :], deg[:, :]))
                link(layer_norm(c, xc))
                for i in range(TC):
                    t = c * TC + i
                    ins = nc.vector.tensor_scalar(U[:, t, :], X[:, t, :], dis[:, t:t + 1], None, ALU.mult)
                ins.then_inc(s_X, 1)
            for c in range(NC):
                k = NC + c
                dve.wait_ge(s_Z, k + 1)
                z = psZ[k % 2].rearrange("p (t d) -> p t d", d=D)
                for i in range(TC):
                    t = c * TC + i
                    ins = nc.vector.scalar_tensor_tensor(out=hid[:, k % 2, i, :], in0=z[:, i, :], scalar=dis[:, t:t + 1],
                                                         in1=X[:, t, :], op0=ALU.mult, op1=ALU.add)
                link(ins)
                layer_norm(k, X[:, c * TC:(c + 1) * TC, :]).then_inc(s_X, 1)
            for c in range(NC):
                k = 2 * NC + c
                dve.wait_ge(s_Z, k + 1)
                xc = X[:, c * TC:(c + 1) * TC, :]
                link(nc.vector.tensor_tensor(fin[:, c * TC:(c + 1) * TC, :].rearrange("p t d -> p (t d)") if False else
                                             U[:, c * TC:(c + 1) * TC, :].rearrange("p t d -> p (t d)"),
                                             psS[c % 2], xc.rearrange("p t d -> p (t d)"), ALU.add))
                z = psZ[k % 2].rearrange("p (t d) -> p t d", d=D)
                for i in range(TC):
                    t = c * TC + i
                    ins = nc.vector.scalar_tensor_tensor(out=hid[:, k % 2, i, :], in0=z[:, i, :], scalar=rdeg[:, t:t + 1],
                                                         in1=U[:, t, :], op0=ALU.mult, op1=ALU.add)
                link(ins)
                layer_norm(k, X[:, c * TC:(c + 1) * TC, :]).then_inc(s_X, 1)
            dve.wait_ge(s_T3c, 2 * NC)
            nc.vector.memset(acc2[:, :, 0], 0.0).then_inc(s_used[0], 1)
            nc.vector.memset(acc2[:, :, 1], 0.0).then_inc(s_used[1], 1)
            with dve.Fori(0, NG) as n:
                with dve.Fori(0, G) as r:
                    for h in range(H):
                        dve.wait_ge(s_bc[h], n * G + r + 1)
                        dve.wait_ge(s_gelu[h], n * G + r + 1)
                        nc.vector.scalar_tensor_tensor(out=junk[:, h, :], in0=gel[:, h, :], scalar=1.0, in1=psB[h][:, :],
                                                       op0=ALU.mult, op1=ALU.mult,
                                                       accum_out=acc2[:, bass.ds(r, 1), h]).then_inc(s_used[h], 1)
                for h in range(H):
                    dve.wait_ge(s_used[h], (n + 1) * G + 1)
                nc.vector.tensor_tensor(accT[:, bass.ds(n * G, G)], acc2[:, :, 0], acc2[:, :, 1], ALU.add).then_inc(s_acc, 1)
                dve.wait_ge(s_acc, n + 1)
            dve.wait_ge(s_bcln, 1)
            link(nc.vector.tensor_copy(lnw_bc[:, :], psB[0][:, 0:D]))
            link(nc.vector.tensor_copy(lnb_bc[:, :], psB[0][:, D:2 * D]))
            for c in range(NC):
                b = c % 2
                k = 3 * NC + 2 * c
                xc = X[:, c * TC:(c + 1) * TC, :]
                dve.wait_ge(s_Fg, c + 1)
                dve.wait_ge(s_X, 3 * NC + c)
                link(nc.vector.tensor_tensor(hid2[:, 0, :, :], upd[:, c * TC:(c + 1) * TC, :], xc, ALU.add))
                link(layer_norm2(dve, link, k, hid2[:, 0, :, :], hid2[:, 1, :, :]))
                link(nc.vector.tensor_tensor(hid2[:, 0, :, :], hid2[:, 1, :, :],
                                             lnw_bc[:, :].unsqueeze(1).to_broadcast([P, TC, D]), ALU.mult))
                link(nc.vector.tensor_tensor(hid2[:, 1, :, :], hid2[:, 0, :, :],
                                             lnb_bc[:, :].unsqueeze(1).to_broadcast([P, TC, D]), ALU.add))
                link(nc.vector.tensor_tensor(hid2[:, 0, :, :], hid2[:, 1, :, :], xc, ALU.add))
                layer_norm2(dve, link, k + 1, hid2[:, 0, :, :], fin[:, c * TC:(c + 1) * TC, :]).then_inc(s_X, 1)

        @block.tensor
        def _(pe):
            pe.wait_ge(s_const, 5)
            pe.wait_ge(s_w, N_W)
            pe.wait_ge(s_x, 16)

            def mm(out_, l, r, start=True, stop=True):
                return nc.tensor.matmul(out_, l, r, start=start, stop=stop)

            def aggregate(l):
                src = (X, U, X)[l]
                if l == 0:
                    for J in range(T):
                        pe.wait_ge(s_adjT[J], 16)
                        for c in range(NC):
                            ins = mm(ps[c][:, :], X[:, J, :], adjT_sb[:, J, c * CW:(c + 1) * CW], J == 0, J == T - 1)
                            if J == T - 1:
                                ins.then_inc(s_Y, 1)
                    return
                pe.wait_ge(s_X, NC * l)
                pe.wait_ge(s_YT, NC * l)
                for J in range(T - 1):
                    for c in range(NC):
                        mm(ps[c][:, :], src[:, J, :], adjT_sb[:, J, c * CW:(c + 1) * CW], J == 0, False)
                for c in range(NC):
                    if l == 1:
                        for i in range(TC):
                            mm(ps[c][:, i * P:(i + 1) * P], U[:, c * TC + i, :], ident[:, :], False, False)
                    mm(ps[c][:, :], src[:, T - 1, :], adjT_sb[:, T - 1, c * CW:(c + 1) * CW], False, True).then_inc(s_Y, 1)

            def project(l, c):
                k = NC * l + c
                pe.wait_ge(s_YT, k + 1)
                if k >= 2:
                    pe.wait_ge(s_X, k - 1)
                w = (W0, W1, WNEIGH)[l]
                for i in range(TC):
                    o = psZ[k % 2][:, i * D:(i + 1) * D]
                    if l == 0:
                        mm(o, ones_row[:, :], rows[:, B0, :], True, False)
                    ins = mm(o, YT[:, k % 2, i * P:(i + 1) * P], wts[:, w, :], l != 0, True)
                    if l == 2:
                        t = c * TC + i
                        ins = mm(psS[c % 2][:, i * D:(i + 1) * D], XT2[:, t * P:(t + 1) * P], wts[:, WSELF, :], True, True)
                ins.then_inc(s_Z, 1)

            def transpose_X(l, c):
                k = NC * l + c
                pe.wait_ge(s_X, NC * (l + 1) + c + 1)
                if k >= 2 and l == 0:
                    pe.wait_ge(s_XT, k - 1)
                for i in range(TC):
                    ins = nc.tensor.transpose((psS[k % 2] if l == 0 else ps[c][:, :])[:, i * P:(i + 1) * P], X[:, c * TC + i, :], ident[:, :])
                ins.then_inc(s_XTp, 1)

            for l in range(3):
                if l == 2:
                    for c in range(NC):
                        transpose_X(0, c)
                    pe.wait_ge(s_XT, NC)
                aggregate(l)
                for c in range(NC):
                    project(l, c)
            for c in range(NC):
                transpose_X(1, c)
            pe.wait_ge(s_XT, 2 * NC)
            for c in range(NC):
                if c:
                    pe.wait_ge(s_T3c, 2 * c - 1)
                mm(psZ[0], wts[:, MDST, :], XT[:, c * CW:(c + 1) * CW]).then_inc(s_T3, 1)
                if c:
                    pe.wait_ge(s_T3c, 2 * c)
                mm(psZ[1], wts[:, MSRC, :], XT[:, c * CW:(c + 1) * CW]).then_inc(s_T3, 1)
            pe.wait_ge(s_T3c, 2 * NC)

            def dense_group(b, n):
                pe.wait_ge(s_split, n + 1)
                pe.sem_inc(s_turn, 1)
                with pe.Fori(0, G) as r:
                    for h in range(H):
                        pe.wait_ge(s_used[h], n * G + r + 1)
                        for q in range(HW // CW):
                            ins = mm(psB[h][:, q * CW:(q + 1) * CW], sel_bf[:, bass.ds(r, 1)].to_broadcast([3 * G, P]),
                                     parts[:, b, h * HW + q * CW:h * HW + (q + 1) * CW])
                        ins.then_inc(s_bc[h], 1)
                pe.wait_ge(s_bc[H - 1], (n + 1) * G)
                pe.sem_inc(s_rowsdone, 1)

            with pe.Fori(0, NG // 2) as m:
                dense_group(0, m * 2)
                dense_group(1, m * 2 + 1)
            pe.wait_ge(s_acc, NG)
            mm(psB[0][:, 0:D], ones_row[:, :], rows[:, LNW, :])
            mm(psB[0][:, D:2 * D], ones_row[:, :], rows[:, LNB, :]).then_inc(s_bcln, 1)
            for c in range(NC):
                for i in range(TC):
                    t = c * TC + i
                    o = ps[c][:, i * D:(i + 1) * D]
                    mm(o, ones_row[:, :], rows[:, UPDB, :], True, False)
                    mm(o, XT[:, t * P:(t + 1) * P], wts[:, UPDX, :], False, False)
                    ins = mm(o, accT[:, t * P:(t + 1) * P], wts[:, UPDA, :], False, True)
                ins.then_inc(s_F, 1)


def kernel(**inputs):
    import numpy as np
    import concourse.bacc as bacc
    from concourse.bass_utils import run_bass_kernel_spmd as run

    a = {k: np.asarray(v) for k, v in inputs.items()}
    mw, uw = a["L3_gnn_msg_w"], a["L3_gnn_upd_w"]
    row = lambda v: v.reshape(1, -1)
    arrays = {
        "x": a["x"], "adj": a["adj"], "adjT": a["adj"].T,
        "w0": a["L0_gnn_kernel"], "b0": row(a["L0_gnn_bias"]), "w1": a["L1_gnn_weight"],
        "w_self": a["L2_gnn_W_self"], "w_neigh": a["L2_gnn_W_neigh"],
        "msg_src": mw[:, :D].T, "msg_dst": mw[:, D:].T, "msg_b": row(a["L3_gnn_msg_b"]),
        "upd_x": uw[:, :D].T, "upd_agg": uw[:, D:].T, "upd_b": row(a["L3_gnn_upd_b"]),
        "ln_w": row(a["L3_gnn_ln_w"]), "ln_b": row(a["L3_gnn_ln_b"]),
    }
    nc = bacc.Bacc("TRN2", target_bir_lowering=False, num_devices=1)
    aps, feed = {}, {}
    for k, v in arrays.items():
        v = np.ascontiguousarray(v)
        feed[f"in_{k}"] = v
        aps[k] = nc.dram_tensor(f"in_{k}", v.shape, mybir.dt.from_np(v.dtype), kind="ExternalInput").ap()
    aps["out"] = nc.dram_tensor("out_0", (N, D), F32, kind="ExternalOutput").ap()
    build(nc, xT_unused=None, **aps)
    r = run(nc, [feed], core_ids=[0])
    return r.results[0]["out_0"]
```

```python
from contextlib import ExitStack

import concourse.bass as bass
from concourse import mybir

ALU = mybir.AluOpType
ACT = mybir.ActivationFunctionType
F32 = mybir.dt.float32
BF16 = mybir.dt.bfloat16
I32 = mybir.dt.int32
U32 = mybir.dt.uint32
AX_X = mybir.AxisListType.X

P = 128
N = 2048
D = 128
T = N // P
NC = 4
CW = N // NC
TC = CW // P
H = 2
HW = N // H
G = 32
NG = N // G
QG = P // G
LN_EPS = 1e-5
DEG_EPS = 1e-6
STAGE = 2

SLOTS = [0, 44, 40, 32, 32, 28, 28] + [24] * 9
SEGS = [0, 32] + [16] * 8 + [8] * 6
MAXC = 8 * max(SEGS)
MAXK = 48
SLOT0 = [sum(SLOTS[:t]) for t in range(T + 1)]
GW = 4
GROUPS = [k // GW for k in SLOTS]
GROUP0 = [sum(GROUPS[:t]) for t in range(T + 1)]
RING = 6
NGROUPS = GROUP0[T]
LATE = 2
UPDATES = {7: 1, 11: 2, T - 2: 0, T - 1: 3}


def build(nc, x, adj, adjT, w0, b0, w1, w_self, w_neigh, msg_src, msg_dst, msg_b,
          upd_x, upd_agg, upd_b, ln_w, ln_b, out):
    ctx = ExitStack()
    with ctx:
        def sb(name, shape, dt=F32):
            return ctx.enter_context(nc.sbuf_tensor(name, shape, dt))

        def sem(name):
            return ctx.enter_context(nc.semaphore(name))

        adjT_sb = sb("adjT_sb", [P, T, N])
        adj_rows = sb("adj_rows", [P, STAGE, N])
        pack_in = sb("pack_in", [P, N])
        X = sb("X", [P, T, D])
        U = sb("U", [P, T, D])
        XT2 = U[:, :, :].rearrange("p t d -> p (t d)")
        hid = sb("hid", [P, 2, TC, D])
        YT = sb("YT", [P, 2, CW])
        wts = sb("wts", [P, 8, D])
        W0, W1, WSELF, WNEIGH, MSRC, MDST, UPDX, UPDA = range(8)
        rows = sb("rows", [1, 5, D])
        B0, MSGB, UPDB, LNW, LNB = range(5)
        msgb_col = sb("msgb_col", [P, 1])
        ones_row = sb("ones_row", [1, P])
        ones_col = sb("ones_col", [P, 1])
        ident = sb("ident", [P, P])
        sel_bf = sb("sel_bf", [P, P], BF16)
        sel_f = sb("sel_f", [P, P])
        zeros_bf = sb("zeros_bf", [P, P], BF16)
        eps_ln = sb("eps_ln", [P, 1])
        eps_deg = sb("eps_deg", [P, 1])
        row_sum = sb("row_sum", [P, T])
        sign_sum = sb("sign_sum", [P, T])
        found = sb("found", [P, T])
        room = sb("room", [P, T])
        bad = sb("bad", [P, 3, T])
        bad_row = sb("bad_row", [P, 1])
        flag_i = sb("flag_i", [1, 1], I32)
        dis = sb("dis", [P, T])
        dis_root = sb("dis_root", [P, T])
        deg = sb("deg", [P, T])
        rdeg = sb("rdeg", [P, T])
        bn6 = sb("bn6", [P, 2, TC, 6])
        mv = sb("mv", [P, 2, TC, 2])
        root = sb("root", [P, 2, TC])
        rstd = sb("rstd", [P, 2, TC])
        lnw_bc = sb("lnw_bc", [P, D])
        lnb_bc = sb("lnb_bc", [P, D])
        xs = sb("xs", [P, HW])
        cand = sb("cand", [P, MAXC])
        cpos = sb("cpos", [P, MAXC], U32)
        seg_f = sb("seg_f", [P, 2, MAXC])
        ckey = sb("ckey", [P, MAXC])
        cwork = sb("cwork", [P, MAXC])
        cjunk = sb("cjunk", [P, 2, MAXC])
        seg_i = cjunk[:, :, :].bitcast(I32)
        keys = sb("keys", [P, MAXK])
        wslot = sb("wslot", [P, SLOT0[T]])
        jslot = sb("jslot", [P, SLOT0[T]], U32)
        parts0 = adj_rows[:, :, :].rearrange("p a n -> p (a n)").bitcast(BF16).rearrange(
            "p (q n) -> p q n", q=QG)
        pool = adjT_sb[:, :, :].rearrange("p t n -> p (t n)")
        XT = pool[:, 0:N]
        dT = pool[:, N:2 * N]
        sT = pool[:, 2 * N:3 * N]
        accT = pool[:, 3 * N:4 * N]
        gel = pool[:, 4 * N:5 * N].rearrange("p (h n) -> p h n", h=H)
        junk = pool[:, 5 * N:6 * N].rearrange("p (h n) -> p h n", h=H)
        fin = pool[:, 6 * N:7 * N].rearrange("p (t n) -> p t n", t=T)
        S = pool[:, 8 * N:9 * N].rearrange("p (t d) -> p t d", t=T)
        Dn = pool[:, 9 * N:10 * N].rearrange("p (t d) -> p t d", t=T)
        GB = GW * D
        edge = pool[:, 10 * N:10 * N + RING * GB].rearrange("p (r s d) -> p r s d", r=RING, s=GW)
        diag = pool[:, 12 * N:12 * N + RING * GB].rearrange("p (r s d) -> p r s d", r=RING, s=GW)
        hid2 = pool[:, 7 * N:8 * N].rearrange("p (a t d) -> p a t d", a=4, t=TC)
        upd = hid2[:, 2, :, :]
        acc2 = pool[:, 14 * N:14 * N + P * H].rearrange("p (r h) -> p r h", h=H)
        f_xs = edge[:, 0:4, :, :].rearrange("p r s d -> p (r s d)")
        f_parts = pool[:, 15 * N:16 * N].bitcast(BF16).rearrange("p (b n) -> p b n", b=2)

        ps = [ctx.enter_context(nc.psum_tensor(f"ps{i}", [P, CW], F32)) for i in range(4)]
        psB = [ctx.enter_context(nc.psum_tensor(f"psB{i}", [P, HW], F32)) for i in range(H)]
        psZ = [psB[0][:, 0:CW], psB[0][:, CW:HW]]
        psS = [psB[1][:, 0:CW], psB[1][:, CW:HW]]
        psE = [ps[0], ps[1]]
        psF = [ps[2], ps[3]]

        table = nc.dram_tensor("msg_dst_rows", (N, D), F32, kind="Internal").ap()

        s_w = sem("weights_landed")
        s_x = sem("x_landed")
        s_adjT = [sem(f"adjT_landed{J}") for J in range(T)]
        s_rows = [sem(f"adj_rows_landed{k}") for k in range(STAGE)]
        s_sign = sem("rows_used")
        s_rowsum = sem("row_sums_done")
        s_const = sem("constants_ready")
        NCONST = 10
        s_dis = sem("dis_ready")
        s_pin = sem("pack_in_landed")
        s_pfree = sem("pack_in_used")
        s_packed = sem("tile_packed")
        s_badp = sem("bad_rows_counted")
        s_badps = sem("bad_count_in_psum")
        s_flag = sem("flag_ready")
        s_dchain = sem("dve_step")
        s_pchain = sem("pool_step")
        s_turn = sem("turn_taken")
        s_Y = sem("Y_chunk_ready")
        s_YT = sem("YT_copied")
        s_Z = sem("Z_ready")
        s_var = sem("variance_ready")
        s_root = sem("root_ready")
        s_X = sem("X_chunk_ready")
        s_XTp = sem("XT_in_psum")
        s_XT = sem("XT_copied")
        s_T3 = sem("message_terms_in_psum")
        s_T3c = sem("message_terms_copied")
        s_tab = sem("table_stored")
        s_xs = sem("xs_landed")
        s_cast = sem("part_cast")
        s_sub = sem("part_subtracted")
        s_fill = [sem(f"group_filled{k}") for k in range(RING)]
        s_bc = [sem(f"adj_row_broadcast{h}") for h in range(H)]
        s_gelu = [sem(f"row_gelu_ready{h}") for h in range(H)]
        s_used = [sem(f"row_half_summed{h}") for h in range(H)]
        s_gath = [sem(f"group_gathered{k}") for k in range(RING)]
        s_diag = sem("diagonals_ready")
        s_edge = sem("edge_gelu_ready")
        s_efree = sem("edges_summed")
        s_tileE = sem("tile_messages_in_psum")
        s_acc = sem("tile_messages_copied")
        s_acc0 = sem("tile0_messages_ready")
        f_start = sem("f_may_start")
        f_F = sem("f_update_in_psum")
        f_Fg = sem("f_update_gelu")
        f_var = sem("f_variance_ready")
        f_root = sem("f_root_ready")
        f_fin = sem("f_chunk_ready")
        f_out = sem("f_out_stored")
        f_land = sem("f_rows_landed")
        f_split = sem("f_parts_ready")
        f_done = sem("f_parts_used")
        f_bc = [sem(f"f_row_broadcast{h}") for h in range(H)]
        f_gelu = [sem(f"f_row_gelu_ready{h}") for h in range(H)]
        f_used = [sem(f"f_row_half_summed{h}") for h in range(H)]
        f_acc = sem("f_group_ready")
        s_bcln = sem("ln_vectors_broadcast")
        s_F = sem("update_in_psum")
        s_Fg = sem("update_gelu")
        s_out = sem("out_stored")

        block = ctx.enter_context(nc.Block())

        wlist = [w0, w1, w_self, w_neigh, msg_src, msg_dst, upd_x, upd_agg]
        rlist = [b0, msg_b, upd_b, ln_w, ln_b]
        N_W = 16 * (len(wlist) + len(rlist) + 1)
        NT3 = 4 * NC

        paired = NGROUPS - GROUPS[T - 1]
        extra = P - paired
        extras = [0] + [extra * t // (T - 2) - extra * (t - 1) // (T - 2) for t in range(1, T - 1)] + [0]
        assert sum(extras) == extra and extra >= 0

        def main_order(step, dense, begin=None, end=None, dense_first=True):
            row = 0
            for t in range(1, T):
                if begin:
                    begin(t)
                for g in range(GROUP0[t], GROUP0[t + 1]):
                    if dense_first and t < T - 1:
                        dense(row)
                    step(t, g % RING, g // RING, g)
                    if not dense_first and t < T - 1:
                        dense(row)
                    row += 1
                for _ in range(extras[t]):
                    dense(row)
                    row += 1
                if end:
                    end(t)

        def read_flag(eng):
            eng.wait_ge(s_flag, 1)
            return eng.value_load(flag_i[0:1, 0:1], min_val=0, max_val=P * T * 3)

        @block.sync
        def _(sp):
            sp.dma_start(X[:, :, :], x.rearrange("(t p) d -> p t d", p=P)).then_inc(s_x, 16)
            for J in range(T):
                sp.dma_start(adjT_sb[:, J, :], adjT[J * P:(J + 1) * P, :]).then_inc(s_adjT[J], 16)
                if J >= STAGE:
                    sp.wait_ge(s_sign, J - STAGE + 1)
                sp.dma_start(adj_rows[:, J % STAGE, :], adj[J * P:(J + 1) * P, :]).then_inc(s_rows[J % STAGE], 16)
            for k in range(QG * H):
                q, h = divmod(k, H)
                if k:
                    sp.wait_ge(s_cast, 3 * k)
                for part in range(4):
                    sp.dma_start(xs[part * G:(part + 1) * G, :], adj[q * G:(q + 1) * G, h * HW:(h + 1) * HW]).then_inc(s_xs, 16)
            for c in range(NC):
                sp.wait_ge(s_T3c, 2 * c + 1)
                sp.dma_start(table.rearrange("(t p) d -> p t d", p=P)[:, c * TC:(c + 1) * TC, :],
                             Dn[:, c * TC:(c + 1) * TC, :]).then_inc(s_tab, 16)
            sp.wait_ge(s_T3c, 2 * NC)
            def store(c, done, landed):
                sp.wait_ge(*done)
                sp.dma_start(out.rearrange("(t p) d -> p t d", p=P)[:, c * TC:(c + 1) * TC, :],
                             fin[:, c * TC:(c + 1) * TC, :]).then_inc(landed, 16)

            def fill(g, t):
                if g >= RING:
                    sp.wait_ge(s_efree, g - RING + 1)
                sp.dma_start(edge[:, g % RING, :, :], S[:, t, :].unsqueeze(1).to_broadcast([P, GW, D])).then_inc(s_fill[g % RING], 16)
            for t in range(1, T):
                for g in range(GROUP0[t], GROUP0[t + 1]):
                    fill(g, t)
            for n, c in enumerate(UPDATES.values()):
                store(c, (s_X, 3 * NC + n + 1), s_out)
            sp.wait_ge(s_out, 16 * NC)
            flag = read_flag(sp)
            with sp.If(flag > 0):
                sp.wait_ge(f_start, 1)
                with sp.Fori(QG, NG) as n:
                    sp.wait_ge(f_split, n - QG + 1)
                    for part in range(4):
                        sp.dma_start(f_xs[part * G:(part + 1) * G, :], adj[bass.ds(n * G, G), :]).then_inc(f_land, 16)
                for c in range(NC):
                    store(c, (f_fin, c + 1), f_out)
                sp.wait_ge(f_out, 16 * NC)

        @block.gpsimd
        def _(pl):
            def load_pack_in(t):
                if t > 1:
                    pl.wait_ge(s_pfree, t - 1)
                pl.dma_start(pack_in[:, :], adj[t * P:(t + 1) * P, :]).then_inc(s_pin, 16)

            load_pack_in(1)
            for m, v in ((ident, 0.0), (sel_f, 0.0)):
                pl.memset(m[:, :], v).then_inc(s_pchain, 1)
            for k, nseg in enumerate((SEGS[1], SEGS[2])):
                pl.iota(seg_i[:, k, 0:8 * nseg], pattern=[[1, nseg], [0, 8]], base=1, channel_multiplier=0).then_inc(s_pchain, 1)
            for m, v in ((ones_row, 1.0), (ones_col, 1.0), (eps_ln, LN_EPS), (eps_deg, DEG_EPS), (zeros_bf, 0.0)):
                pl.memset(m[:, :], v).then_inc(s_const, 1)
            for t in range(1, T):
                ins = pl.memset(room[:, t:t + 1], float(SLOTS[t]))
            ins.then_inc(s_const, 1)
            pl.wait_ge(s_pchain, 4)
            pl.affine_select(out=ident[:, :], in_=ident[:, :], compare_op=ALU.not_equal, fill=1.0,
                             base=0, pattern=[[-1, P]], channel_multiplier=1).then_inc(s_const, 1)
            for k, nseg in enumerate((SEGS[1], SEGS[2])):
                pl.tensor_copy(seg_f[:, k, 0:8 * nseg], seg_i[:, k, 0:8 * nseg]).then_inc(s_const, 1)
            n = 4
            for d in range(-P // G + 1, P // G):
                pl.wait_ge(s_pchain, n)
                pl.affine_select(out=sel_f[:, :], in_=sel_f[:, :], compare_op=ALU.not_equal, fill=1.0,
                                 base=-d * G, pattern=[[-1, P]], channel_multiplier=1).then_inc(s_pchain, 1)
                n += 1
            pl.wait_ge(s_pchain, n)
            pl.memset(sel_f[G:2 * G, :], 0.0).then_inc(s_pchain, 1)
            n += 1
            pl.wait_ge(s_pchain, n)
            pl.tensor_copy(sel_bf[:, :], sel_f[:, :]).then_inc(s_const, 1)

            for t in range(2, 8):
                load_pack_in(t)
            pl.wait_ge(s_sign, T)
            for k in range(QG * H):
                q, h = divmod(k, H)
                pl.wait_ge(s_cast, 3 * k + 1)
                pl.tensor_tensor(xs[:, :], xs[:, :], parts0[:, q, h * HW:(h + 1) * HW], ALU.subtract).then_inc(s_sub, 1)
                pl.wait_ge(s_cast, 3 * k + 2)
                pl.tensor_tensor(xs[3 * G:, :], xs[3 * G:, :], parts0[3 * G:, q, h * HW:(h + 1) * HW], ALU.subtract).then_inc(s_sub, 1)
                if 8 + k <= T - LATE:
                    load_pack_in(8 + k)

            def split(src, dst, n0):
                def after(k):
                    pl.wait_ge(s_pchain, n0 + k)
                    pl.sem_inc(s_turn, 1)
                pl.tensor_copy(dst[:, :], src[:, :]).then_inc(s_pchain, 1)
                after(1)
                pl.tensor_tensor(src[:, :], src[:, :], dst[:, :], ALU.subtract).then_inc(s_pchain, 1)
                after(2)
                pl.tensor_copy(dst[2 * G:, :], src[2 * G:, :]).then_inc(s_pchain, 1)
                after(3)
                pl.tensor_tensor(src[3 * G:, :], src[3 * G:, :], dst[3 * G:, :], ALU.subtract).then_inc(s_pchain, 1)
                after(4)
                pl.tensor_copy(dst[3 * G:, :], src[3 * G:, :]).then_inc(s_pchain, 1)
                after(5)

            pl.wait_ge(s_tab, 16 * NC)
            for t in range(1, T):
                pl.wait_ge(s_packed, t)
                for g in range(GROUP0[t], GROUP0[t + 1]):
                    if 3 <= t < 2 + LATE and g == GROUP0[t] + 3:
                        load_pack_in(T - LATE + t - 2)
                    pl.wait_ge(s_fill[g % RING], 16 * (g // RING + 1))
                    for k in range(GW):
                        pl.indirect_dma_start(edge[:, g % RING, k, :], None, table,
                                              bass.IndirectOffsetOnAxis(ap=jslot[:, g * GW + k:g * GW + k + 1], axis=0),
                                              compute_op=ALU.add).then_inc(s_gath[g % RING], 16)

            flag = read_flag(pl)
            with pl.If(flag > 0):
                pl.sem_inc(f_split, 1)
                with pl.Fori(QG // 2, NG // 2) as m:
                    for b in range(2):
                        k = m * 2 + (b - QG)
                        pl.wait_ge(f_land, k * 64 + 64)
                        pl.wait_ge(f_done, k + 1)
                        pl.sem_inc(s_turn, 1)
                        split(f_xs, f_parts[:, b, :], k * 5 + n)
                        pl.sem_inc(f_split, 1)

        @block.scalar
        def _(act):
            for k, w in enumerate(wlist):
                act.dma_start(wts[:, k, :], w).then_inc(s_w, 16)
            for k, r in enumerate(rlist):
                act.dma_start(rows[:, k, :], r).then_inc(s_w, 16)
            act.dma_start(msgb_col[:, :], msg_b.rearrange("a d -> d a")).then_inc(s_w, 16)
            for t in range(T):
                a = adj_rows[:, t % STAGE, :]
                act.wait_ge(s_rows[t % STAGE], 16 * (t // STAGE + 1))
                act.activation(a, a, ACT.Copy, accum_out=row_sum[:, t:t + 1]).then_inc(s_rowsum, 1)
                act.wait_ge(s_rowsum, t + 1)
                act.activation(a, a, ACT.Sign, accum_out=sign_sum[:, t:t + 1]).then_inc(s_sign, 1)
            act.wait_ge(s_const, NCONST)
            act.activation(dis_root[:, :], row_sum[:, :], ACT.Sqrt, bias=eps_deg[:, :]).then_inc(s_dis, 1)

            def copy_Y(l, c):
                k = NC * l + c
                act.wait_ge(s_Y, k + 1)
                if k >= 2:
                    act.wait_ge(s_Z, k - 1)
                act.activation(YT[:, k % 2, :], ps[c][:, :], ACT.Copy).then_inc(s_YT, 1)

            def roots(k, var=s_var, rt=s_root):
                act.wait_ge(var, k + 1)
                act.activation(root[:, k % 2, :], mv[:, k % 2, :, 1], ACT.Sqrt, bias=eps_ln[:, :]).then_inc(rt, 1)

            def cast_parts(k):
                q, h = divmod(k, H)
                dst = parts0[:, q, h * HW:(h + 1) * HW]
                if k == 0:
                    act.wait_ge(s_sign, T)
                act.wait_ge(s_xs, 64 * (k + 1))
                act.activation(dst, xs[:, :], ACT.Copy).then_inc(s_cast, 1)
                act.wait_ge(s_sub, 2 * k + 1)
                act.activation(dst[2 * G:, :], xs[2 * G:, :], ACT.Copy).then_inc(s_cast, 1)
                act.wait_ge(s_sub, 2 * k + 2)
                act.activation(dst[3 * G:, :], xs[3 * G:, :], ACT.Copy).then_inc(s_cast, 1)

            for l in range(3):
                if l == 2:
                    for c in range(NC):
                        act.wait_ge(s_XTp, c + 1)
                        act.activation(XT2[:, c * CW:(c + 1) * CW], psS[c % 2], ACT.Copy).then_inc(s_XT, 1)
                if l:
                    for k in range(QG):
                        cast_parts((l - 1) * QG + k)
                for c in range(NC):
                    copy_Y(l, c)
                    if c:
                        roots(NC * l + c - 1)
                roots(NC * l + NC - 1)
            for c in range(NC):
                act.wait_ge(s_XTp, NC + c + 1)
                act.activation(XT[:, c * CW:(c + 1) * CW], ps[c][:, :], ACT.Copy).then_inc(s_XT, 1)
            act.preload_act_table(ACT.Gelu)
            for c in range(NC):
                act.wait_ge(s_T3, 2 * c + 1)
                act.activation(Dn[:, c * TC:(c + 1) * TC, :].rearrange("p t d -> p (t d)"), psZ[0], ACT.Copy).then_inc(s_T3c, 1)
                act.wait_ge(s_T3, 2 * c + 2)
                act.activation(S[:, c * TC:(c + 1) * TC, :].rearrange("p t d -> p (t d)"), psZ[1], ACT.Copy).then_inc(s_T3c, 1)
            for c in range(NC):
                act.wait_ge(s_T3, 2 * NC + 2 * c + 1)
                act.activation(dT[:, c * CW:(c + 1) * CW], psZ[0], ACT.Copy).then_inc(s_T3c, 1)
                act.wait_ge(s_T3, 2 * NC + 2 * c + 2)
                act.activation(sT[:, c * CW:(c + 1) * CW], psZ[1], ACT.Identity, bias=msgb_col[:, :]).then_inc(s_T3c, 1)
            act.wait_ge(s_T3c, NT3)

            def row_gelu(r, col, ready, used):
                for h in range(H):
                    act.wait_ge(used[h], r + 1)
                    if not isinstance(r, int):
                        act.sem_inc(s_turn, 1)
                    act.activation(gel[:, h, :], dT[:, h * HW:(h + 1) * HW], ACT.Gelu,
                                   bias=sT[:, bass.ds(col, 1)] if not isinstance(col, int) else sT[:, col:col + 1]).then_inc(ready[h], 1)

            def edge_gelu(t, slot, turn, g):
                act.wait_ge(s_gath[slot], 16 * GW * (turn + 1))
                e = edge[:, slot, :, :].rearrange("p s d -> p (s d)")
                act.activation(e, e, ACT.Gelu).then_inc(s_edge, 1)

            def update(n, k, ready, done, var, rt):
                act.wait_ge(ready, n + 1)
                act.activation(upd.rearrange("p t d -> p (t d)"), psF[n % 2][:, :], ACT.Gelu).then_inc(done, 1)
                act.preload_act_table(ACT.Sqrt)
                for j in range(2):
                    roots(k + j, var, rt)

            def end_tile(t):
                act.wait_ge(s_tileE, t)
                act.activation(accT[:, t * P:(t + 1) * P], psE[t % 2][:, 0:P], ACT.Copy).then_inc(s_acc, 1)
                if t in UPDATES:
                    n = list(UPDATES).index(t)
                    update(n, 3 * NC + 2 * n, s_F, s_Fg, s_var, s_root)
                    if t < T - 1:
                        act.preload_act_table(ACT.Gelu)

            main_order(edge_gelu, lambda r: row_gelu(r, r, s_gelu, s_used), end=end_tile)

            flag = read_flag(act)
            with act.If(flag > 0):
                act.preload_act_table(ACT.Gelu)
                with act.Fori(0, N - P) as r:
                    row_gelu(r, r + P, f_gelu, f_used)
                for n in range(NC):
                    update(n, 2 * n, f_F, f_Fg, f_var, f_root)

        @block.vector
        def _(dve):
            chain = [0]

            def step(ins):
                chain[0] += 1
                ins.then_inc(s_dchain, 1)
                return chain[0]

            def link(ins):
                dve.wait_ge(s_dchain, step(ins))

            def layer_norm(k, src, dst, var=s_var, rt=s_root):
                b = k % 2
                for i in range(TC):
                    ins = nc.vector.bn_stats(out=bn6[:, b, i, :], in_=src[:, i, :])
                link(ins)
                for i in range(TC):
                    ins = nc.vector.bn_aggr(out=mv[:, b, i, :], in_=bn6[:, b, i, :])
                ins.then_inc(var, 1)
                dve.wait_ge(rt, k + 1)
                link(nc.vector.reciprocal(rstd[:, b, :], root[:, b, :]))
                for i in range(TC):
                    ins = nc.vector.tensor_scalar(dst[:, i, :], src[:, i, :], mv[:, b, i, 0:1], rstd[:, b, i:i + 1],
                                                  ALU.subtract, ALU.mult)
                return ins

            def pack(t):
                nseg, K = SEGS[t], SLOTS[t]
                C = 8 * nseg
                c, p, key, work = cand[:, 0:C], cpos[:, 0:C], ckey[:, 0:C], cwork[:, 0:C]
                dve.wait_ge(s_pin, 16 * t)
                for g in range(nseg):
                    ins = nc.vector.max(cand[:, 8 * g:8 * g + 8], pack_in[:, g::nseg])
                link(ins)
                for g in range(nseg):
                    ins = nc.vector.max_index(cpos[:, 8 * g:8 * g + 8], cand[:, 8 * g:8 * g + 8], pack_in[:, g::nseg])
                ins.then_inc(s_pfree, 1)
                dve.wait_ge(s_pfree, t)
                link(nc.vector.scalar_tensor_tensor(out=work, in0=p, scalar=float(nseg), in1=seg_f[:, min(t, 2) - 1, 0:C],
                                                    op0=ALU.mult, op1=ALU.add))
                step(nc.vector.tensor_scalar(cjunk[:, 1, 0:C], c, 0.0, 0.0, ALU.is_gt, ALU.add, accum_out=found[:, t:t + 1]))
                link(nc.vector.scalar_tensor_tensor(out=key, in0=c, scalar=0.0, in1=work, op0=ALU.is_gt, op1=ALU.mult))
                rounds = (K + 7) // 8
                for q in range(rounds):
                    link(nc.vector.max(keys[:, 8 * q:8 * q + 8], key if q == 0 else work))
                    if q < rounds - 1:
                        link(nc.vector.match_replace(work, keys[:, 8 * q:8 * q + 8], key if q == 0 else work, 0.0))
                for k in range(K):
                    if k >= 2:
                        dve.wait_ge(s_dchain, chain[0] - 1)
                    step(nc.vector.scalar_tensor_tensor(out=cjunk[:, k % 2, 0:C], in0=key, scalar=keys[:, k:k + 1], in1=c,
                                                   op0=ALU.is_equal, op1=ALU.mult,
                                                   accum_out=wslot[:, SLOT0[t] + k:SLOT0[t] + k + 1]))
                ins = nc.vector.tensor_scalar(jslot[:, SLOT0[t]:SLOT0[t + 1]], keys[:, 0:K], 1.0, 0.0, ALU.subtract, ALU.max)
                ins.then_inc(s_packed, 1)
                dve.wait_ge(s_packed, t)

            dve.wait_ge(s_x, 16)
            dve.wait_ge(s_const, NCONST)
            for t in range(1, 6):
                pack(t)
            for c in range(NC):
                dve.wait_ge(s_Z, c + 1)
                xc = X[:, c * TC:(c + 1) * TC, :]
                link(nc.vector.scalar_tensor_tensor(out=hid[:, c % 2, :, :].rearrange("p t d -> p (t d)"),
                                                    in0=psZ[c % 2], scalar=0.0,
                                                    in1=xc.rearrange("p t d -> p (t d)"), op0=ALU.max, op1=ALU.add))
                if c == 0:
                    dve.wait_ge(s_dis, 1)
                    link(nc.vector.reciprocal(dis[:, :], dis_root[:, :]))
                    link(nc.vector.tensor_scalar(deg[:, :], row_sum[:, :], 1.0, None, ALU.max))
                    link(nc.vector.reciprocal(rdeg[:, :], deg[:, :]))
                link(layer_norm(c, hid[:, c % 2, :, :], xc))
                for i in range(TC):
                    t = c * TC + i
                    ins = nc.vector.tensor_scalar(U[:, t, :], X[:, t, :], dis[:, t:t + 1], None, ALU.mult)
                ins.then_inc(s_X, 1)
            for t in range(6, 10):
                pack(t)
            for c in range(NC):
                k = NC + c
                dve.wait_ge(s_Z, k + 1)
                z = psZ[k % 2].rearrange("p (t d) -> p t d", d=D)
                for i in range(TC):
                    t = c * TC + i
                    ins = nc.vector.scalar_tensor_tensor(out=hid[:, k % 2, i, :], in0=z[:, i, :], scalar=dis[:, t:t + 1],
                                                         in1=X[:, t, :], op0=ALU.mult, op1=ALU.add)
                link(ins)
                layer_norm(k, hid[:, k % 2, :, :], X[:, c * TC:(c + 1) * TC, :]).then_inc(s_X, 1)
            for t in range(10, 14):
                pack(t)
            for c in range(NC):
                k = 2 * NC + c
                dve.wait_ge(s_Z, k + 1)
                xc = X[:, c * TC:(c + 1) * TC, :]
                link(nc.vector.tensor_tensor(XT2[:, c * CW:(c + 1) * CW],
                                             psS[c % 2], xc.rearrange("p t d -> p (t d)"), ALU.add))
                z = psZ[k % 2].rearrange("p (t d) -> p t d", d=D)
                for i in range(TC):
                    t = c * TC + i
                    ins = nc.vector.scalar_tensor_tensor(out=hid[:, k % 2, i, :], in0=z[:, i, :], scalar=rdeg[:, t:t + 1],
                                                         in1=XT2[:, t * P:(t + 1) * P], op0=ALU.mult, op1=ALU.add)
                link(ins)
                layer_norm(k, hid[:, k % 2, :, :], X[:, c * TC:(c + 1) * TC, :]).then_inc(s_X, 1)
            for t in range(14, T - LATE):
                pack(t)
            def find_incomplete():
                f, sg, rm = found[:, 1:T], sign_sum[:, 1:T], room[:, 1:T]
                dve.wait_ge(s_sign, T)
                nc.vector.tensor_tensor(bad[:, 0, 1:T], f, sg, ALU.not_equal)
                link(nc.vector.tensor_tensor(bad[:, 1, 1:T], f, rm, ALU.is_gt))
                link(nc.vector.tensor_tensor(bad[:, 2, 1:T], bad[:, 0, 1:T], bad[:, 1, 1:T], ALU.add))
                nc.vector.tensor_reduce(bad_row[:, :], bad[:, 2, 1:T], AX_X, ALU.add).then_inc(s_badp, 1)

            dve.wait_ge(s_bcln, 1)
            nc.vector.tensor_copy(lnw_bc[:, :], psF[0][:, 0:D])
            link(nc.vector.tensor_copy(lnb_bc[:, :], psF[0][:, D:2 * D]))
            dve.wait_ge(s_T3c, NT3)
            for h in range(H):
                dve.sem_inc(s_used[h], 1)

            def row_sum_half(r, idx, h, bc, ready, used):
                dve.wait_ge(bc[h], r + 1)
                dve.wait_ge(ready[h], r + 1)
                nc.vector.scalar_tensor_tensor(out=junk[:, h, :], in0=gel[:, h, :], scalar=1.0, in1=psB[h][:, :],
                                               op0=ALU.mult, op1=ALU.mult,
                                               accum_out=acc2[:, idx:idx + 1, h] if isinstance(idx, int) else acc2[:, bass.ds(idx, 1), h]).then_inc(used[h], 1)

            def weights_diag(t, slot, turn, g):
                if g >= RING:
                    dve.wait_ge(s_efree, g - RING + 1)
                nc.vector.tensor_tensor(diag[:, slot, :, :], ident[:, :].unsqueeze(1).to_broadcast([P, GW, P]),
                                        wslot[:, g * GW:(g + 1) * GW].unsqueeze(2).to_broadcast([P, GW, P]),
                                        ALU.mult).then_inc(s_diag, 1)

            def dense(r):
                for h in range(H):
                    row_sum_half(r, r, h, s_bc, s_gelu, s_used)

            def update(n, c, k, done, var, rt, fin_sem):
                xc = X[:, c * TC:(c + 1) * TC, :]
                a, b = hid2[:, 0, :, :], hid2[:, 1, :, :]
                dve.wait_ge(done, n + 1)
                link(nc.vector.tensor_tensor(a, upd, xc, ALU.add))
                link(layer_norm(k, a, b, var, rt))
                link(nc.vector.tensor_tensor(a, b, lnw_bc[:, :].unsqueeze(1).to_broadcast([P, TC, D]), ALU.mult))
                link(nc.vector.tensor_tensor(b, a, lnb_bc[:, :].unsqueeze(1).to_broadcast([P, TC, D]), ALU.add))
                link(nc.vector.tensor_tensor(a, b, xc, ALU.add))
                ins = layer_norm(k + 1, a, fin[:, c * TC:(c + 1) * TC, :], var, rt)
                ins.then_inc(fin_sem[0], 1)
                dve.wait_ge(*fin_sem)

            def end_tile(t):
                if t == T - 2:
                    for h in range(H):
                        dve.wait_ge(s_used[h], P + 1)
                    nc.vector.tensor_tensor(accT[:, 0:P], acc2[:, :, 0], acc2[:, :, 1], ALU.add).then_inc(s_acc0, 1)
                if t in UPDATES:
                    n = list(UPDATES).index(t)
                    update(n, UPDATES[t], 3 * NC + 2 * n, s_Fg, s_var, s_root, (s_X, 3 * NC + n + 1))
                if 2 <= t < 2 + LATE:
                    pack(T - LATE + t - 2)
                if t == 1 + LATE:
                    find_incomplete()
                if t == 4 + LATE:
                    dve.wait_ge(s_badps, 1)
                    nc.vector.tensor_copy(flag_i[:, :], psF[1][0:1, 0:1]).then_inc(s_flag, 1)

            main_order(weights_diag, dense, end=end_tile, dense_first=False)
            flag = read_flag(dve)
            with dve.If(flag > 0):
                dve.sem_inc(f_start, 1)
                for h in range(H):
                    dve.sem_inc(f_used[h], 1)
                with dve.Fori(0, NG - QG) as n:
                    with dve.Fori(0, G) as r:
                        for h in range(H):
                            row_sum_half(n * G + r, r, h, f_bc, f_gelu, f_used)
                    for h in range(H):
                        dve.wait_ge(f_used[h], n * G + (G + 1))
                    nc.vector.tensor_tensor(accT[:, bass.ds(n * G + P, G)], acc2[:, 0:G, 0], acc2[:, 0:G, 1],
                                            ALU.add).then_inc(f_acc, 1)
                    dve.wait_ge(f_acc, n + 1)
                for c in range(NC):
                    update(c, c, 2 * c, f_Fg, f_var, f_root, (f_fin, c + 1))

        @block.tensor
        def _(pe):
            pe.wait_ge(s_const, NCONST)
            pe.wait_ge(s_w, N_W)
            pe.wait_ge(s_x, 16)

            def mm(out_, l, r, start=True, stop=True):
                return nc.tensor.matmul(out_, l, r, start=start, stop=stop)

            def aggregate(l):
                src = (X, U, X)[l]
                if l:
                    pe.wait_ge(s_X, NC * l)
                    pe.wait_ge(s_YT, NC * l)
                for J in range(T):
                    if l == 0:
                        pe.wait_ge(s_adjT[J], 16)
                    for c in range(NC):
                        if J == T - 1 and l == 1:
                            for i in range(TC):
                                mm(ps[c][:, i * P:(i + 1) * P], U[:, c * TC + i, :], ident[:, :], False, False)
                        ins = mm(ps[c][:, :], src[:, J, :], adjT_sb[:, J, c * CW:(c + 1) * CW], J == 0, J == T - 1)
                        if J == T - 1:
                            ins.then_inc(s_Y, 1)

            def project(l, c):
                k = NC * l + c
                pe.wait_ge(s_YT, k + 1)
                if k >= 2:
                    pe.wait_ge(s_X, k - 1)
                w = (W0, W1, WNEIGH)[l]
                for i in range(TC):
                    o = psZ[k % 2][:, i * D:(i + 1) * D]
                    if l == 0:
                        mm(o, ones_row[:, :], rows[:, B0, :], True, False)
                    ins = mm(o, YT[:, k % 2, i * P:(i + 1) * P], wts[:, w, :], l != 0, True)
                    if l == 2:
                        t = c * TC + i
                        ins = mm(psS[c % 2][:, i * D:(i + 1) * D], XT2[:, t * P:(t + 1) * P], wts[:, WSELF, :])
                ins.then_inc(s_Z, 1)

            def transpose_X(l, c):
                pe.wait_ge(s_X, NC * (l + 1) + c + 1)
                if l == 0 and c >= 2:
                    pe.wait_ge(s_XT, c - 1)
                for i in range(TC):
                    ins = nc.tensor.transpose((psS[c % 2] if l == 0 else ps[c][:, :])[:, i * P:(i + 1) * P],
                                              X[:, c * TC + i, :], ident[:, :])
                ins.then_inc(s_XTp, 1)

            for l in range(3):
                if l == 2:
                    for c in range(NC):
                        transpose_X(0, c)
                    pe.wait_ge(s_XT, NC)
                aggregate(l)
                for c in range(NC):
                    project(l, c)
            for c in range(NC):
                transpose_X(1, c)
            pe.wait_ge(s_X, 3 * NC)
            for c in range(NC):
                pe.wait_ge(s_XT, NC + c + 1)
                if c:
                    pe.wait_ge(s_T3c, 2 * c - 1)
                for i in range(TC):
                    t = c * TC + i
                    ins = mm(psZ[0][:, i * D:(i + 1) * D], XT[:, t * P:(t + 1) * P], wts[:, MDST, :])
                ins.then_inc(s_T3, 1)
                if c:
                    pe.wait_ge(s_T3c, 2 * c)
                for i in range(TC):
                    t = c * TC + i
                    mm(psZ[1][:, i * D:(i + 1) * D], ones_row[:, :], rows[:, MSGB, :], True, False)
                    ins = mm(psZ[1][:, i * D:(i + 1) * D], XT[:, t * P:(t + 1) * P], wts[:, MSRC, :], False, True)
                ins.then_inc(s_T3, 1)
            for c in range(NC):
                pe.wait_ge(s_T3c, 2 * NC + 2 * c - 1)
                mm(psZ[0], wts[:, MDST, :], XT[:, c * CW:(c + 1) * CW]).then_inc(s_T3, 1)
                pe.wait_ge(s_T3c, 2 * NC + 2 * c)
                mm(psZ[1], wts[:, MSRC, :], XT[:, c * CW:(c + 1) * CW]).then_inc(s_T3, 1)
            mm(psF[0][:, 0:D], ones_row[:, :], rows[:, LNW, :])
            mm(psF[0][:, D:2 * D], ones_row[:, :], rows[:, LNB, :]).then_inc(s_bcln, 1)
            pe.wait_ge(s_T3c, NT3)
            pe.wait_ge(s_cast, 3 * QG * H)

            def dense(r):
                for h in range(H):
                    pe.wait_ge(s_used[h], r + 1)
                    for q in range(HW // CW):
                        o = h * HW + q * CW
                        ins = mm(psB[h][:, q * CW:(q + 1) * CW], sel_bf[:, r:r + 1].to_broadcast([P, P]),
                                 parts0[:, r // G, o:o + CW])
                    ins.then_inc(s_bc[h], 1)

            def sum_edges(t, slot, turn, g):
                pe.wait_ge(s_diag, g + 1)
                pe.wait_ge(s_edge, g + 1)
                for k in range(GW):
                    ins = mm(psE[t % 2][:, 0:P], edge[:, slot, k, :], diag[:, slot, k, :],
                             g == GROUP0[t] and k == 0, g == GROUP0[t + 1] - 1 and k == GW - 1)
                ins.then_inc(s_efree, 1)
                if g == GROUP0[t + 1] - 1:
                    pe.wait_ge(s_efree, g + 1)
                    pe.sem_inc(s_tileE, 1)

            def update(n, c, done):
                for i in range(TC):
                    t = c * TC + i
                    o = psF[n % 2][:, i * D:(i + 1) * D]
                    mm(o, ones_row[:, :], rows[:, UPDB, :], True, False)
                    mm(o, XT[:, t * P:(t + 1) * P], wts[:, UPDX, :], False, False)
                    ins = mm(o, accT[:, t * P:(t + 1) * P], wts[:, UPDA, :], False, True)
                ins.then_inc(done, 1)

            def begin_tile(t):
                if t > 2:
                    pe.wait_ge(s_acc, t - 2)

            def end_tile(t):
                if t in UPDATES:
                    n = list(UPDATES).index(t)
                    pe.wait_ge(s_acc, t)
                    if t == T - 2:
                        pe.wait_ge(s_acc0, 1)
                    if n == 0:
                        pe.wait_ge(s_bcln, 1)
                    if n:
                        pe.wait_ge(s_X, 3 * NC + n)
                    update(n, UPDATES[t], s_F)
                if t == 3 + LATE:
                    pe.wait_ge(s_badp, 1)
                    mm(psF[1][0:1, 0:1], bad_row[:, :], ones_col[:, :]).then_inc(s_badps, 1)

            main_order(sum_edges, dense, begin_tile, end_tile)

            flag = read_flag(pe)
            with pe.If(flag > 0):
                pe.wait_ge(f_start, 1)
                pe.sem_inc(f_done, 2)
                with pe.Fori(0, (NG - QG) // 2) as m:
                    for b in range(2):
                        pe.wait_ge(f_split, m * 2 + (b + 2))
                        pe.sem_inc(s_turn, 1)
                        with pe.Fori(0, G) as r:
                            for h in range(H):
                                pe.wait_ge(f_used[h], m * (2 * G) + r + (b * G + 1))
                                for q in range(HW // CW):
                                    o = h * HW + q * CW
                                    ins = mm(psB[h][:, q * CW:(q + 1) * CW], sel_bf[:, bass.ds(r, 1)].to_broadcast([P, P]),
                                             f_parts[:, b, o:o + CW])
                                ins.then_inc(f_bc[h], 1)
                        pe.wait_ge(f_bc[H - 1], m * (2 * G) + (b + 1) * G)
                        pe.sem_inc(f_done, 1)
                pe.wait_ge(f_acc, NG - QG)
                for c in range(NC):
                    if c:
                        pe.wait_ge(f_fin, c)
                    update(c, c, f_F)


def kernel(**inputs):
    import numpy as np
    import concourse.bacc as bacc
    from concourse.bass_utils import run_bass_kernel_spmd as run

    a = {k: np.asarray(v) for k, v in inputs.items()}
    mw, uw = a["L3_gnn_msg_w"], a["L3_gnn_upd_w"]
    row = lambda v: v.reshape(1, -1)
    arrays = {
        "x": a["x"], "adj": a["adj"], "adjT": a["adj"].T,
        "w0": a["L0_gnn_kernel"], "b0": row(a["L0_gnn_bias"]), "w1": a["L1_gnn_weight"],
        "w_self": a["L2_gnn_W_self"], "w_neigh": a["L2_gnn_W_neigh"],
        "msg_src": mw[:, :D].T, "msg_dst": mw[:, D:].T, "msg_b": row(a["L3_gnn_msg_b"]),
        "upd_x": uw[:, :D].T, "upd_agg": uw[:, D:].T, "upd_b": row(a["L3_gnn_upd_b"]),
        "ln_w": row(a["L3_gnn_ln_w"]), "ln_b": row(a["L3_gnn_ln_b"]),
    }
    nc = bacc.Bacc("TRN2", target_bir_lowering=False, num_devices=1)
    aps, feed = {}, {}
    for k, v in arrays.items():
        v = np.ascontiguousarray(v)
        feed[f"in_{k}"] = v
        aps[k] = nc.dram_tensor(f"in_{k}", v.shape, mybir.dt.from_np(v.dtype), kind="ExternalInput").ap()
    aps["out"] = nc.dram_tensor("out_0", (N, D), F32, kind="ExternalOutput").ap()
    build(nc, **aps)
    r = run(nc, [feed], core_ids=[0])
    return r.results[0]["out_0"]
```

```python
from contextlib import ExitStack

import concourse.bass as bass
from concourse import mybir

ALU = mybir.AluOpType
ACT = mybir.ActivationFunctionType
F32 = mybir.dt.float32
BF16 = mybir.dt.bfloat16
I32 = mybir.dt.int32
U32 = mybir.dt.uint32
AX_X = mybir.AxisListType.X

P = 128
N = 2048
D = 128
T = N // P
NC = 4
CW = N // NC
TC = CW // P
H = 2
HW = N // H
G = 32
NG = N // G
DR = P - G
QG = DR // G
QV = P // G
FG = 2
LN_EPS = 1e-5
DEG_EPS = 1e-6
JADD = 13

SLOTS = [16, 42, 38, 31, 29, 25, 24, 20, 23, 19, 20, 21, 19, 21, 20, 17]
SEGS = [8] + [16] * 4 + [8] * 11
MAXC = 8 * max(SEGS)
MAXK = 48
SLOT0 = [sum(SLOTS[:t]) for t in range(T + 1)]
GW = 4
GROUPS = [-(-k // GW) for k in SLOTS]
GROUP0 = [sum(GROUPS[:t]) for t in range(T + 1)]
RING = 8
NGROUPS = GROUP0[T]
WIDTH = [min(GW, SLOTS[t] - q * GW) for t in range(T) for q in range(GROUPS[t])]
FIRST = [sum(WIDTH[:g]) for g in range(NGROUPS)]
LATE = 4
LATE0 = 2
PACKS = [(0, 3), (3, 6), (6, 10), (10, T - LATE)]
EARLY = 5
NODES_AFTER = [6, 9, 10, 12]
UPDATES = [(7, 4, 8), (11, 8, 12), (T - 2, 0, 4), (T - 1, 12, T)]


def build(nc, x, adj, adjV, adjT, w0, b0, w1, w_self, w_neigh, msg_src, msg_dst, msg_b,
          upd_x, upd_agg, upd_b, ln_w, ln_b, out):
    ctx = ExitStack()
    with ctx:
        def sb(name, shape, dt=F32):
            return ctx.enter_context(nc.sbuf_tensor(name, shape, dt))

        def sem(name):
            return ctx.enter_context(nc.semaphore(name))

        adjT_sb = sb("adjT_sb", [P, T, N])
        pack_in = sb("pack_in", [P, 2, N])
        parts0 = sb("parts0", [P, QG, N], BF16)
        acc_rows = parts0[:, 0:2, :].rearrange("p q n -> p (q n)").bitcast(F32)
        signs = sb("signs", [P, N], BF16)
        X = sb("X", [P, T, D])
        U = sb("U", [P, T, D])
        XT2 = U[:, :, :].rearrange("p t d -> p (t d)")
        hid = sb("hid", [P, 2, TC, D])
        YT = sb("YT", [P, 2, CW])
        wts = sb("wts", [P, 8, D])
        W0, W1, WSELF, WNEIGH, MSRC, MDST, UPDX, UPDA = range(8)
        rows = sb("rows", [1, 5, D])
        B0, MSGB, UPDB, LNW, LNB = range(5)
        msgb_col = sb("msgb_col", [P, 1])
        ones_row = sb("ones_row", [1, P])
        ones_col = sb("ones_col", [P, 1])
        ident = sb("ident", [P, P])
        sel_bf = sb("sel_bf", [P, P], BF16)
        sel_f = sb("sel_f", [P, P])
        quarter = sb("quarter", [P, 1])
        eps_ln = sb("eps_ln", [P, 1])
        eps_deg = sb("eps_deg", [P, 1])
        row_sum = sb("row_sum", [P, T])
        nonzeros = sb("nonzeros", [P, T])
        found = sb("found", [P, T])
        twice = sb("twice", [P, T])
        room = sb("room", [P, T])
        bad = sb("bad", [P, 3, T])
        bad_row = sb("bad_row", [P, 1])
        flag_i = sb("flag_i", [1, 1], I32)
        dis = sb("dis", [P, T])
        dis_root = sb("dis_root", [P, T])
        deg = sb("deg", [P, T])
        rdeg = sb("rdeg", [P, T])
        bn6 = sb("bn6", [P, 2, TC, 6])
        mv = sb("mv", [P, 2, TC, 2])
        root = sb("root", [P, 2, TC])
        rstd = sb("rstd", [P, 2, TC])
        lnw_bc = sb("lnw_bc", [P, D])
        lnb_bc = sb("lnb_bc", [P, D])
        xs = sb("xs", [P, HW])
        cand = sb("cand", [P, MAXC])
        cpos = sb("cpos", [P, MAXC], U32)
        seg_f = sb("seg_f", [P, MAXC])
        ckey = sb("ckey", [P, MAXC])
        cwork = sb("cwork", [P, MAXC])
        cjunk = sb("cjunk", [P, 2, MAXC])
        seg_i = cjunk[:, 0, :].bitcast(I32)
        keys = sb("keys", [P, MAXK])
        wslot = sb("wslot", [P, SLOT0[T]])
        jslot = sb("jslot", [P, SLOT0[T]], U32)
        pool = adjT_sb[:, :, :].rearrange("p t n -> p (t n)")
        XT = pool[:, 0:N]
        dT = pool[:, N:2 * N]
        sT = pool[:, 2 * N:3 * N]
        accT = pool[:, 3 * N:4 * N]
        gel = pool[:, 4 * N:5 * N].rearrange("p (h n) -> p h n", h=H)
        junk = pool[:, 5 * N:6 * N].rearrange("p (h n) -> p h n", h=H)
        fin = pool[:, 6 * N:7 * N].rearrange("p (t n) -> p t n", t=T)
        S = pool[:, 8 * N:9 * N].rearrange("p (t d) -> p t d", t=T)
        Dn = pool[:, 9 * N:10 * N].rearrange("p (t d) -> p t d", t=T)
        GB = GW * D
        edge = pool[:, 10 * N:10 * N + RING * GB].rearrange("p (r s d) -> p r s d", r=RING, s=GW)
        diag = pool[:, 12 * N:12 * N + RING * GB].rearrange("p (r s d) -> p r s d", r=RING, s=GW)
        hid2 = pool[:, 7 * N:8 * N].rearrange("p (a t d) -> p a t d", a=4, t=TC)
        upd = hid2[:, 2, :, :]
        acc2 = pool[:, 14 * N:14 * N + P * H].rearrange("p (r h) -> p r h", h=H)
        SV = pool[:, 15 * N - D:15 * N]
        f_xs = edge[:, 0:4, :, :].rearrange("p r s d -> p (r s d)")
        f_parts = pool[:, 15 * N:16 * N].bitcast(BF16).rearrange("p (b n) -> p b n", b=2)

        ps = [ctx.enter_context(nc.psum_tensor(f"ps{i}", [P, CW], F32)) for i in range(4)]
        psB = [ctx.enter_context(nc.psum_tensor(f"psB{i}", [P, HW], F32)) for i in range(H)]
        psZ = [psB[0][:, 0:CW], psB[0][:, CW:HW]]
        psS = [psB[1][:, 0:CW], psB[1][:, CW:HW]]
        psE = [ps[0], ps[1]]
        psF = [ps[2], ps[3]]

        table = nc.dram_tensor("msg_dst_rows", (N, D), F32, kind="Internal").ap()

        s_w = sem("weights_landed")
        s_x = sem("x_landed")
        s_adjT = [sem(f"adjT_landed{J}") for J in range(T)]
        s_accrow = sem("adjT_tile_added")
        s_accall = sem("adjT_added_up")
        s_zfree = sem("Z_bank_read")
        s_Dn = sem("Dn_in_psum")
        s_Dnc = sem("Dn_copied")
        s_rs = sem("row_sums_in_psum")
        s_rowsum = sem("row_sums_ready")
        s_sign = sem("signs_taken")
        s_count = sem("nonzeros_counted")
        s_SV = sem("entry0_terms_landed")
        s_const = sem("constants_ready")
        NCONST = 8
        s_dis = sem("dis_ready")
        s_pin = [sem(f"pack_in_landed{b}") for b in range(2)]
        s_pfree = sem("pack_in_used")
        s_packed = sem("tile_packed")
        s_badp = sem("bad_rows_counted")
        s_badps = sem("bad_count_in_psum")
        s_flag = sem("flag_ready")
        s_dchain = sem("dve_step")
        s_pchain = sem("pool_step")
        s_turn = sem("turn_taken")
        s_Y = sem("Y_chunk_ready")
        s_YT = sem("YT_copied")
        s_Z = sem("Z_ready")
        s_var = sem("variance_ready")
        s_root = sem("root_ready")
        s_X = sem("X_chunk_ready")
        s_XTp = sem("XT_in_psum")
        s_XT = sem("XT_copied")
        s_T3 = sem("message_terms_in_psum")
        s_T3c = sem("message_terms_copied")
        s_tab = sem("table_stored")
        s_xs = sem("xs_landed")
        s_cast = sem("part_cast")
        s_sub = sem("part_subtracted")
        s_fill = [sem(f"group_filled{k}") for k in range(RING)]
        s_bc = [sem(f"adj_row_broadcast{h}") for h in range(H)]
        s_gelu = [sem(f"row_gelu_ready{h}") for h in range(H)]
        s_used = [sem(f"row_half_summed{h}") for h in range(H)]
        s_gath = [sem(f"group_gathered{k}") for k in range(RING)]
        s_diag = sem("diagonals_ready")
        s_edge = sem("edge_gelu_ready")
        s_efree = sem("edges_summed")
        s_tileE = sem("tile_messages_in_psum")
        s_acc = sem("tile_messages_copied")
        s_acc0 = sem("tile0_messages_ready")
        f_start = sem("f_may_start")
        f_F = sem("f_update_in_psum")
        f_Fg = sem("f_update_gelu")
        f_var = sem("f_variance_ready")
        f_root = sem("f_root_ready")
        f_fin = sem("f_chunk_ready")
        f_out = sem("f_out_stored")
        f_land = sem("f_rows_landed")
        f_split = sem("f_parts_ready")
        f_done = sem("f_parts_used")
        f_bc = [sem(f"f_row_broadcast{h}") for h in range(H)]
        f_gelu = [sem(f"f_row_gelu_ready{h}") for h in range(H)]
        f_used = [sem(f"f_row_half_summed{h}") for h in range(H)]
        f_acc = sem("f_group_ready")
        s_bcln = sem("ln_vectors_broadcast")
        s_F = sem("update_in_psum")
        s_Fg = sem("update_gelu")
        s_out = sem("out_stored")

        block = ctx.enter_context(nc.Block())

        wlist = [w0, w1, w_self, w_neigh, msg_src, msg_dst, upd_x, upd_agg]
        rlist = [b0, msg_b, upd_b, ln_w, ln_b]
        N_W = 16 * (len(wlist) + len(rlist) + 1)
        NT3 = 3 * NC

        assert NGROUPS - GROUPS[T - 1] >= DR

        def main_order(step, dense, begin=None, end=None, dense_first=True):
            for t in range(T):
                if begin:
                    begin(t)
                for g in range(GROUP0[t], GROUP0[t + 1]):
                    if dense_first and g < DR:
                        dense(g)
                    step(t, g % RING, g // RING, g)
                    if not dense_first and g < DR:
                        dense(g)
                if end:
                    end(t)

        def load_pack_in(eng, t):
            if t >= 2:
                eng.wait_ge(s_pfree, t - 1)
                eng.wait_ge(s_sign, t - 1)
            if t == 0:
                eng.dma_start(pack_in[:, 0, 0:N // QV], adjV).then_inc(s_pin[0], 16)
            else:
                eng.dma_start(pack_in[:, t % 2, :], adj[t * P:(t + 1) * P, :]).then_inc(s_pin[t % 2], 16)

        def read_flag(eng):
            eng.wait_ge(s_flag, 1)
            return eng.value_load(flag_i[0:1, 0:1], min_val=0, max_val=P * T * (MAXK + 2))

        @block.sync
        def _(sp):
            sp.dma_start(X[:, :, :], x.rearrange("(t p) d -> p t d", p=P)).then_inc(s_x, 16)
            for J in range(T):
                if J >= 3:
                    sp.wait_ge(s_adjT[J - 3], 16)
                sp.dma_start(adjT_sb[:, J, :], adjT[J * P:(J + 1) * P, :]).then_inc(s_adjT[J], 16)
            for t in range(EARLY, PACKS[3][0] + 2):
                load_pack_in(sp, t)
            for c in range(NC):
                sp.wait_ge(s_Dnc, c + 1)
                sp.dma_start(table.rearrange("(t p) d -> p t d", p=P)[:, c * TC:(c + 1) * TC, :],
                             Dn[:, c * TC:(c + 1) * TC, :]).then_inc(s_tab, 16)
                if c == 0:
                    sp.wait_ge(s_T3c, 1)
                    for q in range(QV):
                        sp.dma_start(SV[q * G:(q + 1) * G, :], S[P - G:, 0, :]).then_inc(s_SV, 16)
            sp.wait_ge(s_SV, 16 * QV)
            def store(a, b, done, landed):
                sp.wait_ge(*done)
                sp.dma_start(out.rearrange("(t p) d -> p t d", p=P)[:, a:b, :], fin[:, a:b, :]).then_inc(landed, 16)

            def fill(g, t):
                if g >= RING:
                    sp.wait_ge(s_efree, g - RING + 1)
                s = S[:, t, :] if t else SV
                sp.dma_start(edge[:, g % RING, 0:WIDTH[g], :], s.unsqueeze(1).to_broadcast([P, WIDTH[g], D])).then_inc(s_fill[g % RING], 16)
            for t in range(T):
                if t % TC == 0:
                    sp.wait_ge(s_T3c, t // TC + 1)
                for g in range(GROUP0[t], GROUP0[t + 1]):
                    if t == 1 and 5 <= g - GROUP0[t] < 7:
                        load_pack_in(sp, T - LATE + g - GROUP0[t] - 5)
                    if LATE0 + 1 <= t < LATE0 + LATE - 1 and g == GROUP0[t] + 3:
                        load_pack_in(sp, T - LATE + t - LATE0 + 1)
                    fill(g, t)
            for n, (_, a, b) in enumerate(UPDATES):
                store(a, b, (s_X, 3 * NC + n + 1), s_out)
            sp.wait_ge(s_out, 16 * len(UPDATES))
            flag = read_flag(sp)
            with sp.If(flag > 0):
                sp.wait_ge(f_start, 1)
                with sp.Fori(FG, NG) as n:
                    sp.wait_ge(f_split, n - FG + 1)
                    for part in range(4):
                        sp.dma_start(f_xs[part * G:(part + 1) * G, :], adj[bass.ds(n * G, G), :]).then_inc(f_land, 16)
                for c in range(NC):
                    store(c * TC, (c + 1) * TC, (f_fin, c + 1), f_out)
                sp.wait_ge(f_out, 16 * NC)

        @block.gpsimd
        def _(pl):
            for m, v in ((ident, 0.0), (sel_f, 0.0)):
                pl.memset(m[:, :], v).then_inc(s_pchain, 1)
            pl.iota(seg_i, pattern=[[1, max(SEGS)], [0, 8]], base=1, channel_multiplier=0).then_inc(s_pchain, 1)
            for m, v in ((ones_row, 1.0), (ones_col, 1.0), (eps_ln, LN_EPS), (eps_deg, DEG_EPS)):
                pl.memset(m[:, :], v).then_inc(s_const, 1)
            for t in range(T):
                ins = pl.memset(room[:, t:t + 1], float(SLOTS[t]))
            ins.then_inc(s_const, 1)
            pl.wait_ge(s_pchain, 3)
            pl.affine_select(out=ident[:, :], in_=ident[:, :], compare_op=ALU.not_equal, fill=1.0,
                             base=0, pattern=[[-1, P]], channel_multiplier=1).then_inc(s_const, 1)
            pl.tensor_copy(seg_f[:, :], seg_i).then_inc(s_const, 1)
            n = 3
            for d in range(-P // G + 1, P // G):
                pl.wait_ge(s_pchain, n)
                pl.affine_select(out=sel_f[:, :], in_=sel_f[:, :], compare_op=ALU.not_equal, fill=1.0,
                                 base=-d * G, pattern=[[-1, P]], channel_multiplier=1).then_inc(s_pchain, 1)
                n += 1
            pl.wait_ge(s_pchain, n)
            pl.tensor_copy(sel_bf[:, :], sel_f[:, :]).then_inc(s_pchain, 1)
            n += 1
            pl.wait_ge(s_pchain, n)
            pl.memset(sel_bf[G:2 * G, :], 0.0).then_inc(s_pchain, 1)
            n += 1
            for q in range(QV):
                pl.wait_ge(s_pchain, n)
                pl.memset(quarter[q * G:(q + 1) * G, :], float(q)).then_inc(s_pchain, 1)
                n += 1
            pl.wait_ge(s_pchain, n)
            pl.sem_inc(s_const, 1)

            pl.wait_ge(s_adjT[0], 16)
            for J in range(1, JADD):
                pl.wait_ge(s_adjT[J], 16)
                if J > 1:
                    pl.wait_ge(s_accrow, J - 1)
                pl.tensor_tensor(acc_rows, adjT_sb[:, 0, :] if J == 1 else acc_rows, adjT_sb[:, J, :], ALU.add).then_inc(s_accrow, 1)

            for k in range(QG * H):
                q, h = divmod(k, H)
                if k:
                    pl.wait_ge(s_cast, 3 * k)
                for part in range(4):
                    pl.dma_start(xs[part * G:(part + 1) * G, :], adj[q * G:(q + 1) * G, h * HW:(h + 1) * HW]).then_inc(s_xs, 16)
                pl.wait_ge(s_cast, 3 * k + 1)
                pl.tensor_tensor(xs[:, :], xs[:, :], parts0[:, q, h * HW:(h + 1) * HW], ALU.subtract).then_inc(s_sub, 1)
                pl.wait_ge(s_cast, 3 * k + 2)
                pl.tensor_tensor(xs[3 * G:, :], xs[3 * G:, :], parts0[3 * G:, q, h * HW:(h + 1) * HW], ALU.subtract).then_inc(s_sub, 1)

            def split(src, dst, n0):
                def after(k):
                    pl.wait_ge(s_pchain, n0 + k)
                    pl.sem_inc(s_turn, 1)
                pl.tensor_copy(dst[:, :], src[:, :]).then_inc(s_pchain, 1)
                after(1)
                pl.tensor_tensor(src[:, :], src[:, :], dst[:, :], ALU.subtract).then_inc(s_pchain, 1)
                after(2)
                pl.tensor_copy(dst[2 * G:, :], src[2 * G:, :]).then_inc(s_pchain, 1)
                after(3)
                pl.tensor_tensor(src[3 * G:, :], src[3 * G:, :], dst[3 * G:, :], ALU.subtract).then_inc(s_pchain, 1)
                after(4)
                pl.tensor_copy(dst[3 * G:, :], src[3 * G:, :]).then_inc(s_pchain, 1)
                after(5)

            pl.wait_ge(s_tab, 16 * NC)
            for t in range(T):
                pl.wait_ge(s_packed, t + 1)
                for g in range(GROUP0[t], GROUP0[t + 1]):
                    pl.wait_ge(s_fill[g % RING], 16 * (g // RING + 1))
                    for k in range(WIDTH[g]):
                        pl.indirect_dma_start(edge[:, g % RING, k, :], None, table,
                                              bass.IndirectOffsetOnAxis(ap=jslot[:, FIRST[g] + k:FIRST[g] + k + 1], axis=0),
                                              compute_op=ALU.add).then_inc(s_gath[g % RING], 16)

            flag = read_flag(pl)
            with pl.If(flag > 0):
                pl.sem_inc(f_split, 1)
                with pl.Fori(FG // 2, NG // 2) as m:
                    for b in range(2):
                        k = m * 2 + (b - FG)
                        pl.wait_ge(f_land, k * 64 + 64)
                        pl.wait_ge(f_done, k + 1)
                        pl.sem_inc(s_turn, 1)
                        split(f_xs, f_parts[:, b, :], k * 5 + n)
                        pl.sem_inc(f_split, 1)

        @block.scalar
        def _(act):
            for t in range(2):
                load_pack_in(act, t)
            for k, w in enumerate(wlist):
                act.dma_start(wts[:, k, :], w).then_inc(s_w, 16)
            for k, r in enumerate(rlist):
                act.dma_start(rows[:, k, :], r).then_inc(s_w, 16)
            act.dma_start(msgb_col[:, :], msg_b.rearrange("a d -> d a")).then_inc(s_w, 16)

            def count_nonzeros(t):
                w = N if t else N // QV
                act.wait_ge(s_pin[t % 2], 16 * (t // 2 + 1))
                if t:
                    act.wait_ge(s_count, t)
                act.activation(signs[:, 0:w], pack_in[:, t % 2, 0:w], ACT.Sign).then_inc(s_sign, 1)
                act.wait_ge(s_sign, t + 1)
                act.activation(signs[:, 0:w], signs[:, 0:w], ACT.Square, accum_out=nonzeros[:, t:t + 1]).then_inc(s_count, 1)

            act.wait_ge(s_const, NCONST)

            def copy_Y(l, c):
                k = NC * l + c
                act.wait_ge(s_Y, k + 1)
                if k >= 2:
                    act.wait_ge(s_Z, k - 1)
                act.activation(YT[:, k % 2, :], ps[c][:, :], ACT.Copy).then_inc(s_YT, 1)

            def roots(k, var=s_var, rt=s_root, nt=TC):
                act.wait_ge(var, k + 1)
                act.activation(root[:, k % 2, 0:nt], mv[:, k % 2, 0:nt, 1], ACT.Sqrt, bias=eps_ln[:, :]).then_inc(rt, 1)

            def cast_parts(k):
                q, h = divmod(k, H)
                dst = parts0[:, q, h * HW:(h + 1) * HW]
                act.wait_ge(s_xs, 64 * (k + 1))
                act.activation(dst, xs[:, :], ACT.Copy).then_inc(s_cast, 1)
                act.wait_ge(s_sub, 2 * k + 1)
                act.activation(dst[2 * G:, :], xs[2 * G:, :], ACT.Copy).then_inc(s_cast, 1)
                act.wait_ge(s_sub, 2 * k + 2)
                act.activation(dst[3 * G:, :], xs[3 * G:, :], ACT.Copy).then_inc(s_cast, 1)

            def message_terms(c):
                act.wait_ge(s_XTp, NC + c + 1)
                act.activation(XT[:, c * CW:(c + 1) * CW], ps[c % 2][:, :], ACT.Copy).then_inc(s_XT, 1)
                act.wait_ge(s_Dn, c + 1)
                act.activation(Dn[:, c * TC:(c + 1) * TC, :].rearrange("p t d -> p (t d)"), ps[2][:, :], ACT.Copy).then_inc(s_Dnc, 1)
                if c == 0:
                    act.wait_ge(s_T3, 1)
                    act.activation(S[:, 0:TC, :].rearrange("p t d -> p (t d)"), ps[3][:, :], ACT.Copy).then_inc(s_T3c, 1)

            for l in range(3):
                casts = (l - 1) * (QG * H // 2)
                for t in range(*PACKS[l]):
                    count_nonzeros(t)
                    if t + 2 < EARLY:
                        load_pack_in(act, t + 2)
                    k = t - PACKS[l][0]
                    if l and k < QG * H // 2:
                        cast_parts(casts + k)
                    if l == 2 and k < NC:
                        act.wait_ge(s_XTp, k + 1)
                        act.activation(XT2[:, k * CW:(k + 1) * CW], psS[k % 2], ACT.Copy).then_inc(s_XT, 1)
                copy_Y(l, 0)
                copy_Y(l, 1)
                copy_Y(l, 2)
                roots(NC * l)
                if l == 0:
                    act.wait_ge(s_rs, 1)
                    act.activation(row_sum[:, :], psS[1][:, 0:T], ACT.Copy).then_inc(s_rowsum, 1)
                    act.wait_ge(s_rowsum, 1)
                    act.activation(dis_root[:, :], row_sum[:, :], ACT.Sqrt, bias=eps_deg[:, :]).then_inc(s_dis, 1)
                copy_Y(l, 3)
                for c in range(1, NC):
                    roots(NC * l + c)
                    if l == 2:
                        message_terms(c - 1)
            message_terms(NC - 1)
            act.preload_act_table(ACT.Gelu)
            for n in range(1, 3 * NC):
                act.wait_ge(s_T3, n + 1)
                bank = psZ[n % 2]
                if n < NC:
                    act.activation(S[:, n * TC:(n + 1) * TC, :].rearrange("p t d -> p (t d)"), bank, ACT.Copy).then_inc(s_T3c, 1)
                else:
                    c, src = divmod(n - NC, 2)
                    if src:
                        act.activation(sT[:, c * CW:(c + 1) * CW], bank, ACT.Identity, bias=msgb_col[:, :]).then_inc(s_T3c, 1)
                    else:
                        act.activation(dT[:, c * CW:(c + 1) * CW], bank, ACT.Copy).then_inc(s_T3c, 1)
            for t in range(*PACKS[3]):
                count_nonzeros(t)
            act.wait_ge(s_T3c, NT3)

            def row_gelu(r, col, ready, used):
                for h in range(H):
                    act.wait_ge(used[h], r + 1)
                    if not isinstance(r, int):
                        act.sem_inc(s_turn, 1)
                    act.activation(gel[:, h, :], dT[:, h * HW:(h + 1) * HW], ACT.Gelu,
                                   bias=sT[:, bass.ds(col, 1)] if not isinstance(col, int) else sT[:, col:col + 1]).then_inc(ready[h], 1)

            def edge_gelu(t, slot, turn, g):
                act.wait_ge(s_gath[slot], 16 * sum(WIDTH[g % RING:g + 1:RING]))
                e = edge[:, slot, 0:WIDTH[g], :].rearrange("p s d -> p (s d)")
                act.activation(e, e, ACT.Gelu).then_inc(s_edge, 1)

            def update(n, nt, k, ready, done, var, rt):
                act.wait_ge(ready, n + 1)
                act.activation(upd[:, 0:nt, :].rearrange("p t d -> p (t d)"), psF[n % 2][:, 0:nt * D], ACT.Gelu).then_inc(done, 1)
                act.preload_act_table(ACT.Sqrt)
                for j in range(2):
                    roots(k + j, var, rt, nt)

            def end_tile(t):
                act.wait_ge(s_tileE, t + 1)
                a, b = (t * P, (t + 1) * P) if t else (P - G, P)
                act.activation(accT[:, a:b], psE[t % 2][:, 0:b - a], ACT.Copy).then_inc(s_acc, 1)
                if LATE0 <= t < LATE0 + LATE:
                    count_nonzeros(T - LATE + t - LATE0)
                for n, (after, a, b) in enumerate(UPDATES):
                    if after == t:
                        update(n, b - a, 3 * NC + 2 * n, s_F, s_Fg, s_var, s_root)
                        if n < len(UPDATES) - 1:
                            act.preload_act_table(ACT.Gelu)

            main_order(edge_gelu, lambda r: row_gelu(r, r, s_gelu, s_used), end=end_tile)

            flag = read_flag(act)
            with act.If(flag > 0):
                act.preload_act_table(ACT.Gelu)
                with act.Fori(0, (NG - FG) * G) as r:
                    row_gelu(r, r + FG * G, f_gelu, f_used)
                for n in range(NC):
                    update(n, TC, 2 * n, f_F, f_Fg, f_var, f_root)

        @block.vector
        def _(dve):
            chain = [0]

            def step(ins):
                chain[0] += 1
                ins.then_inc(s_dchain, 1)
                return chain[0]

            def link(ins):
                dve.wait_ge(s_dchain, step(ins))

            def moments(k, src, var=s_var, nt=TC):
                b = k % 2
                for i in range(nt):
                    ins = nc.vector.bn_stats(out=bn6[:, b, i, :], in_=src[:, i, :])
                link(ins)
                for i in range(nt):
                    ins = nc.vector.bn_aggr(out=mv[:, b, i, :], in_=bn6[:, b, i, :])
                ins.then_inc(var, 1)

            def normalise(k, src, dst, rt=s_root, nt=TC):
                b = k % 2
                dve.wait_ge(rt, k + 1)
                link(nc.vector.reciprocal(rstd[:, b, 0:nt], root[:, b, 0:nt]))
                for i in range(nt):
                    ins = nc.vector.tensor_scalar(dst[:, i, :], src[:, i, :], mv[:, b, i, 0:1], rstd[:, b, i:i + 1],
                                                  ALU.subtract, ALU.mult)
                return ins

            def norms(l, residual, scaled=False):
                for c in range(NC + 1):
                    k = NC * l + c
                    if c < NC:
                        dve.wait_ge(s_Z, k + 1)
                        if k >= 2:
                            dve.wait_ge(s_X, k - 1)
                        link(residual(c, k))
                        dve.sem_inc(s_zfree, 1)
                        moments(k, hid[:, k % 2, :, :])
                    if c:
                        c, k = c - 1, k - 1
                        ins = normalise(k, hid[:, k % 2, :, :], X[:, c * TC:(c + 1) * TC, :])
                        if scaled:
                            link(ins)
                            if c == 0:
                                dve.wait_ge(s_dis, 1)
                                step(nc.vector.reciprocal(dis[:, :], dis_root[:, :]))
                                link(nc.vector.tensor_scalar(deg[:, :], row_sum[:, :], 1.0, None, ALU.max))
                                link(nc.vector.reciprocal(rdeg[:, :], deg[:, :]))
                            for i in range(TC):
                                t = c * TC + i
                                ins = nc.vector.tensor_scalar(U[:, t, :], X[:, t, :], dis[:, t:t + 1], None, ALU.mult)
                        ins.then_inc(s_X, 1)

            def pack(t):
                nseg, K = SEGS[t], SLOTS[t]
                C = 8 * nseg
                c, p, key, work = cand[:, 0:C], cpos[:, 0:C], ckey[:, 0:C], cwork[:, 0:C]
                src = pack_in[:, t % 2, 0:(N if t else N // QV)]
                dve.wait_ge(s_pin[t % 2], 16 * (t // 2 + 1))
                for g in range(nseg):
                    ins = nc.vector.max(cand[:, 8 * g:8 * g + 8], src[:, g::nseg])
                link(ins)
                for g in range(nseg):
                    ins = nc.vector.max_index(cpos[:, 8 * g:8 * g + 8], cand[:, 8 * g:8 * g + 8], src[:, g::nseg])
                ins.then_inc(s_pfree, 1)
                dve.wait_ge(s_pfree, t + 1)
                link(nc.vector.scalar_tensor_tensor(out=work, in0=p, scalar=float(nseg), in1=seg_f[:, 0:C],
                                                    op0=ALU.mult, op1=ALU.add))
                step(nc.vector.tensor_scalar(cjunk[:, 1, 0:C], c, 0.0, 0.0, ALU.is_gt, ALU.add, accum_out=found[:, t:t + 1]))
                link(nc.vector.scalar_tensor_tensor(out=key, in0=c, scalar=0.0, in1=work, op0=ALU.is_gt, op1=ALU.mult))
                rounds = (K + 7) // 8
                for q in range(rounds):
                    link(nc.vector.max(keys[:, 8 * q:8 * q + 8], key if q == 0 else work))
                    if q < rounds - 1:
                        link(nc.vector.match_replace(work, keys[:, 8 * q:8 * q + 8], key if q == 0 else work, 0.0))
                link(nc.vector.scalar_tensor_tensor(out=cjunk[:, 0, 0:K - 1], in0=keys[:, 0:K - 1], scalar=0.5,
                                                    in1=keys[:, 1:K], op0=ALU.max, op1=ALU.is_equal,
                                                    accum_out=twice[:, t:t + 1]))
                for k in range(K):
                    if k >= 2:
                        dve.wait_ge(s_dchain, chain[0] - 1)
                    step(nc.vector.scalar_tensor_tensor(out=cjunk[:, k % 2, 0:C], in0=key, scalar=keys[:, k:k + 1], in1=c,
                                                   op0=ALU.is_equal, op1=ALU.mult,
                                                   accum_out=wslot[:, SLOT0[t] + k:SLOT0[t] + k + 1]))
                j = jslot[:, SLOT0[t]:SLOT0[t + 1]]
                if t:
                    ins = nc.vector.tensor_scalar(j, keys[:, 0:K], 1.0, 0.0, ALU.subtract, ALU.max)
                else:
                    link(nc.vector.tensor_scalar(work[:, 0:K], keys[:, 0:K], 1.0, 0.0, ALU.subtract, ALU.max))
                    ins = nc.vector.tensor_scalar(j, work[:, 0:K], float(QV), quarter[:, :], ALU.mult, ALU.add)
                ins.then_inc(s_packed, 1)
                dve.wait_ge(s_packed, t + 1)

            dve.wait_ge(s_x, 16)
            dve.wait_ge(s_const, NCONST)
            for t in range(*PACKS[0]):
                pack(t)
            u = U[:, :, :].rearrange("p t d -> p (t d)")
            for J in range(JADD + 1, T):
                dve.wait_ge(s_adjT[J - 1], 16)
                dve.wait_ge(s_adjT[J], 16)
                link(nc.vector.tensor_tensor(u, adjT_sb[:, JADD, :] if J == JADD + 1 else u, adjT_sb[:, J, :], ALU.add))
            dve.wait_ge(s_accrow, JADD - 1)
            nc.vector.tensor_tensor(acc_rows, acc_rows, u, ALU.add).then_inc(s_accall, 1)
            dve.wait_ge(s_accall, 1)

            def relu_add(c, k):
                ins = nc.vector.scalar_tensor_tensor(out=hid[:, k % 2, :, :].rearrange("p t d -> p (t d)"),
                                                     in0=psZ[k % 2], scalar=0.0,
                                                     in1=X[:, c * TC:(c + 1) * TC, :].rearrange("p t d -> p (t d)"),
                                                     op0=ALU.max, op1=ALU.add)
                return ins

            def dis_add(c, k):
                z = psZ[k % 2].rearrange("p (t d) -> p t d", d=D)
                for i in range(TC):
                    t = c * TC + i
                    ins = nc.vector.scalar_tensor_tensor(out=hid[:, k % 2, i, :], in0=z[:, i, :], scalar=dis[:, t:t + 1],
                                                         in1=X[:, t, :], op0=ALU.mult, op1=ALU.add)
                return ins

            def self_add(c, k):
                link(nc.vector.tensor_tensor(XT2[:, c * CW:(c + 1) * CW], psS[c % 2],
                                             X[:, c * TC:(c + 1) * TC, :].rearrange("p t d -> p (t d)"), ALU.add))
                z = psZ[k % 2].rearrange("p (t d) -> p t d", d=D)
                for i in range(TC):
                    t = c * TC + i
                    ins = nc.vector.scalar_tensor_tensor(out=hid[:, k % 2, i, :], in0=z[:, i, :], scalar=rdeg[:, t:t + 1],
                                                         in1=XT2[:, t * P:(t + 1) * P], op0=ALU.mult, op1=ALU.add)
                return ins

            norms(0, relu_add, scaled=True)
            for t in range(*PACKS[1]):
                pack(t)
            norms(1, dis_add)
            for t in range(*PACKS[2]):
                pack(t)
            norms(2, self_add)
            for t in range(*PACKS[3]):
                pack(t)

            def find_incomplete():
                f, nz, rm = found[:, :], nonzeros[:, :], room[:, :]
                dve.wait_ge(s_count, T)
                nc.vector.tensor_tensor(bad[:, 0, :], f, nz, ALU.not_equal)
                link(nc.vector.tensor_tensor(bad[:, 1, :], f, rm, ALU.is_gt))
                link(nc.vector.tensor_tensor(bad[:, 2, :], bad[:, 0, :], bad[:, 1, :], ALU.add))
                link(nc.vector.tensor_tensor(bad[:, 0, :], bad[:, 2, :], twice[:, :], ALU.add))
                nc.vector.tensor_reduce(bad_row[:, :], bad[:, 0, :], AX_X, ALU.add).then_inc(s_badp, 1)

            dve.wait_ge(s_bcln, 1)
            nc.vector.tensor_copy(lnw_bc[:, :], psF[0][:, 0:D])
            link(nc.vector.tensor_copy(lnb_bc[:, :], psF[0][:, D:2 * D]))
            dve.wait_ge(s_T3c, NT3)
            for h in range(H):
                dve.sem_inc(s_used[h], 1)

            def row_sum_half(r, idx, h, bc, ready, used):
                dve.wait_ge(bc[h], r + 1)
                dve.wait_ge(ready[h], r + 1)
                nc.vector.scalar_tensor_tensor(out=junk[:, h, :], in0=gel[:, h, :], scalar=1.0, in1=psB[h][:, :],
                                               op0=ALU.mult, op1=ALU.mult,
                                               accum_out=acc2[:, idx:idx + 1, h] if isinstance(idx, int) else acc2[:, bass.ds(idx, 1), h]).then_inc(used[h], 1)

            def weights_diag(t, slot, turn, g):
                if g >= RING:
                    dve.wait_ge(s_efree, g - RING + 1)
                n, f = WIDTH[g], FIRST[g]
                w = P if t else G
                nc.vector.tensor_tensor(diag[:, slot, 0:n, 0:w], (ident if t else sel_f)[:, 0:w].unsqueeze(1).to_broadcast([P, n, w]),
                                        wslot[:, f:f + n].unsqueeze(2).to_broadcast([P, n, w]),
                                        ALU.mult).then_inc(s_diag, 1)

            def dense(r):
                for h in range(H):
                    row_sum_half(r, r, h, s_bc, s_gelu, s_used)

            def update(n, t0, t1, k, done, var, rt, fin_sem):
                nt = t1 - t0
                xc = X[:, t0:t1, :]
                a, b = hid2[:, 0, 0:nt, :], hid2[:, 1, 0:nt, :]
                dve.wait_ge(done, n + 1)
                link(nc.vector.tensor_tensor(a, upd[:, 0:nt, :], xc, ALU.add))
                moments(k, a, var, nt)
                link(normalise(k, a, b, rt, nt))
                link(nc.vector.tensor_tensor(a, b, lnw_bc[:, :].unsqueeze(1).to_broadcast([P, nt, D]), ALU.mult))
                link(nc.vector.tensor_tensor(b, a, lnb_bc[:, :].unsqueeze(1).to_broadcast([P, nt, D]), ALU.add))
                link(nc.vector.tensor_tensor(a, b, xc, ALU.add))
                moments(k + 1, a, var, nt)
                normalise(k + 1, a, fin[:, t0:t1, :], rt, nt).then_inc(fin_sem[0], 1)
                dve.wait_ge(*fin_sem)

            def end_tile(t):
                if t == T - 2:
                    for h in range(H):
                        dve.wait_ge(s_used[h], DR + 1)
                    nc.vector.tensor_tensor(accT[:, 0:DR], acc2[:, 0:DR, 0], acc2[:, 0:DR, 1], ALU.add).then_inc(s_acc0, 1)
                for n, (after, a, b) in enumerate(UPDATES):
                    if after == t:
                        update(n, a, b, 3 * NC + 2 * n, s_Fg, s_var, s_root, (s_X, 3 * NC + n + 1))
                if LATE0 <= t < LATE0 + LATE:
                    pack(T - LATE + t - LATE0)
                if t == LATE0 + LATE:
                    find_incomplete()
                if t == LATE0 + LATE + 2:
                    dve.wait_ge(s_badps, 1)
                    nc.vector.tensor_copy(flag_i[:, :], psF[1][0:1, 0:1]).then_inc(s_flag, 1)

            main_order(weights_diag, dense, end=end_tile, dense_first=False)
            flag = read_flag(dve)
            with dve.If(flag > 0):
                dve.sem_inc(f_start, 1)
                for h in range(H):
                    dve.sem_inc(f_used[h], 1)
                with dve.Fori(0, NG - FG) as n:
                    with dve.Fori(0, G) as r:
                        for h in range(H):
                            row_sum_half(n * G + r, r, h, f_bc, f_gelu, f_used)
                    for h in range(H):
                        dve.wait_ge(f_used[h], n * G + (G + 1))
                    nc.vector.tensor_tensor(accT[:, bass.ds(n * G + FG * G, G)], acc2[:, 0:G, 0], acc2[:, 0:G, 1],
                                            ALU.add).then_inc(f_acc, 1)
                    dve.wait_ge(f_acc, n + 1)
                for c in range(NC):
                    update(c, c * TC, (c + 1) * TC, 2 * c, f_Fg, f_var, f_root, (f_fin, c + 1))

        @block.tensor
        def _(pe):
            pe.wait_ge(s_const, NCONST)
            pe.wait_ge(s_x, 16)

            def mm(out_, l, r, start=True, stop=True):
                return nc.tensor.matmul(out_, l, r, start=start, stop=stop)

            def aggregate(l):
                src = (X, U, X)[l]
                if l:
                    pe.wait_ge(s_YT, NC * l)
                for J in range(T):
                    if l == 0:
                        pe.wait_ge(s_adjT[J], 16)
                    elif J % TC == 0:
                        pe.wait_ge(s_X, NC * (l - 1) + J // TC + 1)
                        if l == 2:
                            transpose_X2(J // TC)
                    for c in range(NC):
                        if J == T - 1 and l == 1:
                            for i in range(TC):
                                mm(ps[c][:, i * P:(i + 1) * P], U[:, c * TC + i, :], ident[:, :], False, False)
                        ins = mm(ps[c][:, :], src[:, J, :], adjT_sb[:, J, c * CW:(c + 1) * CW], J == 0, J == T - 1)
                        if J == T - 1:
                            ins.then_inc(s_Y, 1)

            def project(l, c):
                k = NC * l + c
                if k == 0:
                    pe.wait_ge(s_w, N_W)
                pe.wait_ge(s_YT, k + 1)
                if k >= 2:
                    pe.wait_ge(s_zfree, k - 1)
                if l == 2 and c == 0:
                    pe.wait_ge(s_XT, NC)
                w = (W0, W1, WNEIGH)[l]
                for i in range(TC):
                    o = psZ[k % 2][:, i * D:(i + 1) * D]
                    if l == 0:
                        mm(o, ones_row[:, :], rows[:, B0, :], True, False)
                    ins = mm(o, YT[:, k % 2, i * P:(i + 1) * P], wts[:, w, :], l != 0, True)
                    if l == 2:
                        t = c * TC + i
                        ins = mm(psS[c % 2][:, i * D:(i + 1) * D], XT2[:, t * P:(t + 1) * P], wts[:, WSELF, :])
                ins.then_inc(s_Z, 1)

            def transpose_X(bank, c):
                for i in range(TC):
                    ins = nc.tensor.transpose(bank[:, i * P:(i + 1) * P], X[:, c * TC + i, :], ident[:, :])
                ins.then_inc(s_XTp, 1)

            def transpose_X2(c):
                if c >= 2:
                    pe.wait_ge(s_XT, c - 1)
                transpose_X(psS[c % 2], c)

            for l in range(3):
                aggregate(l)
                for c in range(NC):
                    project(l, c)
                    if l == 0 and c == 1:
                        pe.wait_ge(s_accall, 1)
                        for t in range(T):
                            ins = mm(psS[1][:, t:t + 1], acc_rows[:, t * P:(t + 1) * P], ones_col[:, :])
                        ins.then_inc(s_rs, 1)

            def source_by_rows(bank, c):
                for i in range(TC):
                    t = c * TC + i
                    mm(bank[:, i * D:(i + 1) * D], ones_row[:, :], rows[:, MSGB, :], True, False)
                    ins = mm(bank[:, i * D:(i + 1) * D], XT[:, t * P:(t + 1) * P], wts[:, MSRC, :], False, True)
                ins.then_inc(s_T3, 1)

            for c in range(NC):
                pe.wait_ge(s_X, 2 * NC + c + 1)
                if c >= 2:
                    pe.wait_ge(s_XT, NC + c - 1)
                transpose_X(ps[c % 2], c)
                pe.wait_ge(s_XT, NC + c + 1)
                if c:
                    pe.wait_ge(s_Dnc, c)
                for i in range(TC):
                    t = c * TC + i
                    ins = mm(ps[2][:, i * D:(i + 1) * D], XT[:, t * P:(t + 1) * P], wts[:, MDST, :])
                ins.then_inc(s_Dn, 1)
                if c == 0:
                    source_by_rows(ps[3], 0)
            for n in range(1, 3 * NC):
                if n >= 3:
                    pe.wait_ge(s_T3c, n - 1)
                if n < NC:
                    source_by_rows(psZ[n % 2], n)
                else:
                    c, src = divmod(n - NC, 2)
                    mm(psZ[n % 2], wts[:, MSRC if src else MDST, :], XT[:, c * CW:(c + 1) * CW]).then_inc(s_T3, 1)
            pe.wait_ge(s_Dnc, NC)
            mm(psF[0][:, 0:D], ones_row[:, :], rows[:, LNW, :])
            mm(psF[0][:, D:2 * D], ones_row[:, :], rows[:, LNB, :]).then_inc(s_bcln, 1)
            pe.wait_ge(s_T3c, NT3)
            pe.wait_ge(s_cast, 3 * QG * H)

            def dense(r):
                for h in range(H):
                    pe.wait_ge(s_used[h], r + 1)
                    for q in range(HW // CW):
                        o = h * HW + q * CW
                        ins = mm(psB[h][:, q * CW:(q + 1) * CW], sel_bf[:, r:r + 1].to_broadcast([P, P]),
                                 parts0[:, r // G, o:o + CW])
                    ins.then_inc(s_bc[h], 1)

            def sum_edges(t, slot, turn, g):
                pe.wait_ge(s_diag, g + 1)
                pe.wait_ge(s_edge, g + 1)
                w = P if t else G
                for k in range(WIDTH[g]):
                    ins = mm(psE[t % 2][:, 0:w], edge[:, slot, k, :], diag[:, slot, k, 0:w],
                             g == GROUP0[t] and k == 0, g == GROUP0[t + 1] - 1 and k == WIDTH[g] - 1)
                ins.then_inc(s_efree, 1)
                if g == GROUP0[t + 1] - 1:
                    pe.wait_ge(s_efree, g + 1)
                    pe.sem_inc(s_tileE, 1)

            def update_nodes(n, t0, t1):
                for i, t in enumerate(range(t0, t1)):
                    o = psF[n % 2][:, i * D:(i + 1) * D]
                    mm(o, ones_row[:, :], rows[:, UPDB, :], i == 0, False)
                    mm(o, XT[:, t * P:(t + 1) * P], wts[:, UPDX, :], False, False)

            def update_messages(n, t0, t1, done):
                for i, t in enumerate(range(t0, t1)):
                    if t == T - 1 and done is s_F:
                        pe.wait_ge(s_acc, T)
                    ins = mm(psF[n % 2][:, i * D:(i + 1) * D], accT[:, t * P:(t + 1) * P], wts[:, UPDA, :], False, t == t1 - 1)
                ins.then_inc(done, 1)

            def begin_tile(t):
                if t >= 2:
                    pe.wait_ge(s_acc, t - 1)

            def end_tile(t):
                for n, (after, a, b) in enumerate(UPDATES):
                    if after != t:
                        continue
                    pe.wait_ge(s_acc, min(t + 1, T - 1))
                    if t == T - 2:
                        pe.wait_ge(s_acc0, 1)
                    if n:
                        pe.wait_ge(s_X, 3 * NC + n)
                    update_messages(n, a, b, s_F)
                for n, (_, a, b) in enumerate(UPDATES):
                    if t == NODES_AFTER[n]:
                        if n == 1:
                            pe.wait_ge(s_flag, 1)
                        if n >= 2:
                            pe.wait_ge(s_Fg, n - 1)
                        update_nodes(n, a, b)
                if t == LATE0 + LATE + 1:
                    pe.wait_ge(s_badp, 1)
                    mm(psF[1][0:1, 0:1], bad_row[:, :], ones_col[:, :]).then_inc(s_badps, 1)

            main_order(sum_edges, dense, begin_tile, end_tile)

            flag = read_flag(pe)
            with pe.If(flag > 0):
                pe.wait_ge(f_start, 1)
                pe.sem_inc(f_done, 2)
                with pe.Fori(0, (NG - FG) // 2) as m:
                    for b in range(2):
                        pe.wait_ge(f_split, m * 2 + (b + 2))
                        pe.sem_inc(s_turn, 1)
                        with pe.Fori(0, G) as r:
                            for h in range(H):
                                pe.wait_ge(f_used[h], m * (2 * G) + r + (b * G + 1))
                                for q in range(HW // CW):
                                    o = h * HW + q * CW
                                    ins = mm(psB[h][:, q * CW:(q + 1) * CW], sel_bf[:, bass.ds(r, 1)].to_broadcast([P, P]),
                                             f_parts[:, b, o:o + CW])
                                ins.then_inc(f_bc[h], 1)
                        pe.wait_ge(f_bc[H - 1], m * (2 * G) + (b + 1) * G)
                        pe.sem_inc(f_done, 1)
                pe.wait_ge(f_acc, NG - FG)
                for c in range(NC):
                    if c:
                        pe.wait_ge(f_fin, c)
                    update_nodes(c, c * TC, (c + 1) * TC)
                    update_messages(c, c * TC, (c + 1) * TC, f_F)


def kernel(**inputs):
    import numpy as np
    import concourse.bacc as bacc
    from concourse.bass_utils import run_bass_kernel_spmd as run

    a = {k: np.asarray(v) for k, v in inputs.items()}
    mw, uw = a["L3_gnn_msg_w"], a["L3_gnn_upd_w"]
    row = lambda v: v.reshape(1, -1)
    arrays = {
        "x": a["x"], "adj": a["adj"], "adjT": a["adj"].T,
        "adjV": a["adj"][P - G:P].reshape(G, N // QV, QV).transpose(2, 0, 1).reshape(P, N // QV),
        "w0": a["L0_gnn_kernel"], "b0": row(a["L0_gnn_bias"]), "w1": a["L1_gnn_weight"],
        "w_self": a["L2_gnn_W_self"], "w_neigh": a["L2_gnn_W_neigh"],
        "msg_src": mw[:, :D].T, "msg_dst": mw[:, D:].T, "msg_b": row(a["L3_gnn_msg_b"]),
        "upd_x": uw[:, :D].T, "upd_agg": uw[:, D:].T, "upd_b": row(a["L3_gnn_upd_b"]),
        "ln_w": row(a["L3_gnn_ln_w"]), "ln_b": row(a["L3_gnn_ln_b"]),
    }
    nc = bacc.Bacc("TRN2", target_bir_lowering=False, num_devices=1)
    aps, feed = {}, {}
    for k, v in arrays.items():
        v = np.ascontiguousarray(v)
        feed[f"in_{k}"] = v
        aps[k] = nc.dram_tensor(f"in_{k}", v.shape, mybir.dt.from_np(v.dtype), kind="ExternalInput").ap()
    aps["out"] = nc.dram_tensor("out_0", (N, D), F32, kind="ExternalOutput").ap()
    build(nc, **aps)
    r = run(nc, [feed], core_ids=[0])
    return r.results[0]["out_0"]
```
